# Optimizing a Trainium2 kernel written in Bass

```python
import numpy as np
import jax
import jax.numpy as jnp

def _softmax(x, axis=-1):
    return jax.nn.softmax(x, axis=axis)

def _gelu(x):
    return jax.nn.gelu(x, approximate=True)

def _silu(x):
    return jax.nn.silu(x)

def _sigmoid(x):
    return jax.nn.sigmoid(x)

def _layernorm(x, axis=-1, eps=1e-05):
    m = jnp.mean(x, axis=axis, keepdims=True)
    v = jnp.var(x, axis=axis, keepdims=True)
    return (x - m) / jnp.sqrt(v + eps)

def _scatter_add(tgt, idx, src, axis=0):
    return tgt.at[idx].add(src)

def _segment_sum(src, seg, n):
    return jax.ops.segment_sum(src, seg, n)
kernel_name = 'mk_seq_preln_d2_jaxref_r4_9c5523'

def setup_inputs(seed: int=0):
    np.random.seed(seed)
    _w = jnp.asarray

    def _L0_attn_setup():
        import jax, jax.numpy as jnp
        import numpy as np
        EMBED_DIM = 256
        NUM_HEADS = 16
        HEAD_DIM = EMBED_DIM // NUM_HEADS
        B, S = (2, 512)
        key = jax.random.key(seed)
        ks = jax.random.split(key, 9)
        scale = 1.0 / np.sqrt(EMBED_DIM)
        x = jax.random.normal(ks[0], (B, S, EMBED_DIM), dtype=jnp.float32)
        Wq = jax.random.uniform(ks[1], (EMBED_DIM, EMBED_DIM), jnp.float32, -scale, scale)
        bq = jax.random.uniform(ks[2], (EMBED_DIM,), jnp.float32, -scale, scale)
        Wk = jax.random.uniform(ks[3], (EMBED_DIM, EMBED_DIM), jnp.float32, -scale, scale)
        bk = jax.random.uniform(ks[4], (EMBED_DIM,), jnp.float32, -scale, scale)
        Wv = jax.random.uniform(ks[5], (EMBED_DIM, EMBED_DIM), jnp.float32, -scale, scale)
        bv = jax.random.uniform(ks[6], (EMBED_DIM,), jnp.float32, -scale, scale)
        Wo = jax.random.uniform(ks[7], (EMBED_DIM, EMBED_DIM), jnp.float32, -scale, scale)
        bo = jax.random.uniform(ks[8], (EMBED_DIM,), jnp.float32, -scale, scale)
        return {'x': x, 'Wq': Wq, 'bq': bq, 'Wk': Wk, 'bk': bk, 'Wv': Wv, 'bv': bv, 'Wo': Wo, 'bo': bo}
    _L0_attn_in = _L0_attn_setup()

    def _L0_ffn_setup():
        import jax, jax.numpy as jnp
        import numpy as np
        DIM = 256

        def _reference_tuple_inner(x, W_r, W_k, W_v, mu_r, mu_k):
            B, T, C = x.shape
            x_prev = jnp.concatenate([jnp.zeros((B, 1, C), x.dtype), x[:, :-1, :]], axis=1)
            xr = mu_r * x + (1.0 - mu_r) * x_prev
            xk = mu_k * x + (1.0 - mu_k) * x_prev
            r = jax.nn.sigmoid(jnp.einsum('btc,dc->btd', xr, W_r))
            k = jnp.einsum('btc,dc->btd', xk, W_k)
            k_act = jnp.square(jax.nn.relu(k))
            out = r * jnp.einsum('btc,dc->btd', k_act, W_v)
            new_state = x[:, -1, :]
            return (out, new_state)
        key = jax.random.key(seed)
        ks = jax.random.split(key, 6)
        B, T, C = (8, 512, DIM)
        x = jax.random.normal(ks[0], (B, T, C), dtype=jnp.float32)
        s = 1.0 / np.sqrt(C)
        W_r = jax.random.uniform(ks[1], (C, C), jnp.float32, -s, s)
        W_k = jax.random.uniform(ks[2], (C, C), jnp.float32, -s, s)
        W_v = jax.random.uniform(ks[3], (C, C), jnp.float32, -s, s)
        mu_r = jax.random.uniform(ks[4], (C,), jnp.float32)
        mu_k = jax.random.uniform(ks[5], (C,), jnp.float32)
        return {'x': x, 'W_r': W_r, 'W_k': W_k, 'W_v': W_v, 'mu_r': mu_r, 'mu_k': mu_k}
    _L0_ffn_in = _L0_ffn_setup()

    def _L1_attn_setup():
        import math
        import jax, jax.numpy as jnp
        import numpy as np
        D_MODEL = 256
        N_HEADS = 16
        HEAD_DIM = D_MODEL // N_HEADS
        B, L = (1, 1024)

        def _slopes(n_heads):
            ratio = 2.0 ** (-8.0 / n_heads)
            return jnp.asarray([ratio ** (i + 1) for i in range(n_heads)], dtype=jnp.float32)
        key = jax.random.key(seed)
        ks = jax.random.split(key, 5)
        scale = 1.0 / math.sqrt(D_MODEL)
        return {'x': jax.random.normal(ks[0], (B, L, D_MODEL), dtype=jnp.float32), 'q_w': jax.random.normal(ks[1], (D_MODEL, D_MODEL), dtype=jnp.float32) * scale, 'k_w': jax.random.normal(ks[2], (D_MODEL, D_MODEL), dtype=jnp.float32) * scale, 'v_w': jax.random.normal(ks[3], (D_MODEL, D_MODEL), dtype=jnp.float32) * scale, 'o_w': jax.random.normal(ks[4], (D_MODEL, D_MODEL), dtype=jnp.float32) * scale}
    _L1_attn_in = _L1_attn_setup()

    def _L1_ffn_setup():
        import jax, jax.numpy as jnp
        import numpy as np
        from jax import lax
        T, B, I, M, O = (64, 64, 256, 256, 256)

        def _xavier(key, shape):
            fan_out, fan_in = shape
            limit = float(np.sqrt(6.0 / (fan_in + fan_out)))
            return jax.random.uniform(key, shape, jnp.float32, -limit, limit)
        key = jax.random.key(seed)
        ks = jax.random.split(key, 9)
        x = jax.random.normal(ks[0], (T, B, I), jnp.float32)
        return {'x': x, 'wf': _xavier(ks[1], (M, I)), 'uf': _xavier(ks[2], (M, M)), 'bf': jnp.zeros((M,), jnp.float32), 'wi': _xavier(ks[3], (M, I)), 'ui': _xavier(ks[4], (M, M)), 'bi': jnp.zeros((M,), jnp.float32), 'wc': _xavier(ks[5], (M, I)), 'uc': _xavier(ks[6], (M, M)), 'bc': jnp.zeros((M,), jnp.float32), 'wo': _xavier(ks[7], (O, I)), 'uo': _xavier(ks[8], (O, M)), 'bo': jnp.zeros((O,), jnp.float32), 'in_c': jnp.zeros((M,), jnp.float32)}
    _L1_ffn_in = _L1_ffn_setup()
    _d = {'L0_attn_x': _L0_attn_in['x'], 'L0_attn_Wq': _L0_attn_in['Wq'], 'L0_attn_bq': _L0_attn_in['bq'], 'L0_attn_Wk': _L0_attn_in['Wk'], 'L0_attn_bk': _L0_attn_in['bk'], 'L0_attn_Wv': _L0_attn_in['Wv'], 'L0_attn_bv': _L0_attn_in['bv'], 'L0_attn_Wo': _L0_attn_in['Wo'], 'L0_attn_bo': _L0_attn_in['bo'], 'L0_ffn_W_r': _L0_ffn_in['W_r'], 'L0_ffn_W_k': _L0_ffn_in['W_k'], 'L0_ffn_W_v': _L0_ffn_in['W_v'], 'L0_ffn_mu_r': _L0_ffn_in['mu_r'], 'L0_ffn_mu_k': _L0_ffn_in['mu_k'], 'L1_attn_q_w': _L1_attn_in['q_w'], 'L1_attn_k_w': _L1_attn_in['k_w'], 'L1_attn_v_w': _L1_attn_in['v_w'], 'L1_attn_o_w': _L1_attn_in['o_w'], 'L1_ffn_wf': _L1_ffn_in['wf'], 'L1_ffn_uf': _L1_ffn_in['uf'], 'L1_ffn_bf': _L1_ffn_in['bf'], 'L1_ffn_wi': _L1_ffn_in['wi'], 'L1_ffn_ui': _L1_ffn_in['ui'], 'L1_ffn_bi': _L1_ffn_in['bi'], 'L1_ffn_wc': _L1_ffn_in['wc'], 'L1_ffn_uc': _L1_ffn_in['uc'], 'L1_ffn_bc': _L1_ffn_in['bc'], 'L1_ffn_wo': _L1_ffn_in['wo'], 'L1_ffn_uo': _L1_ffn_in['uo'], 'L1_ffn_bo': _L1_ffn_in['bo'], 'L1_ffn_in_c': _L1_ffn_in['in_c']}
    _x0 = _d['L0_attn_x']
    _d['L0_attn_x'] = jax.random.normal(jax.random.fold_in(jax.random.key(seed), 1), (16, 512, 256), dtype=_x0.dtype)
    del _x0
    return _d

def reference(L0_attn_x, L0_attn_Wq, L0_attn_bq, L0_attn_Wk, L0_attn_bk, L0_attn_Wv, L0_attn_bv, L0_attn_Wo, L0_attn_bo, L0_ffn_W_r, L0_ffn_W_k, L0_ffn_W_v, L0_ffn_mu_r, L0_ffn_mu_k, L1_attn_q_w, L1_attn_k_w, L1_attn_v_w, L1_attn_o_w, L1_ffn_wf, L1_ffn_uf, L1_ffn_bf, L1_ffn_wi, L1_ffn_ui, L1_ffn_bi, L1_ffn_wc, L1_ffn_uc, L1_ffn_bc, L1_ffn_wo, L1_ffn_uo, L1_ffn_bo, L1_ffn_in_c):

    def _L0_attn_ref(x, Wq, bq, Wk, bk, Wv, bv, Wo, bo):
        import jax, jax.numpy as jnp
        import numpy as np
        EMBED_DIM = 256
        NUM_HEADS = 16
        HEAD_DIM = EMBED_DIM // NUM_HEADS
        B, S = (2, 512)
        b, s, _ = x.shape
        q = (x @ Wq + bq).reshape(b, s, NUM_HEADS, HEAD_DIM).transpose(0, 2, 1, 3)
        k = (x @ Wk + bk).reshape(b, s, NUM_HEADS, HEAD_DIM).transpose(0, 2, 1, 3)
        v = (x @ Wv + bv).reshape(b, s, NUM_HEADS, HEAD_DIM).transpose(0, 2, 1, 3)
        scores = jnp.einsum('bhqd,bhkd->bhqk', q, k) / jnp.sqrt(jnp.float32(HEAD_DIM))
        weights = jax.nn.softmax(scores, axis=-1)
        out = jnp.einsum('bhqk,bhkd->bhqd', weights, v)
        out = out.transpose(0, 2, 1, 3).reshape(b, s, EMBED_DIM)
        return out @ Wo + bo

    def _L0_ffn_ref(x, W_r, W_k, W_v, mu_r, mu_k):
        import jax, jax.numpy as jnp
        import numpy as np
        DIM = 256

        def _reference_tuple_inner(x, W_r, W_k, W_v, mu_r, mu_k):
            B, T, C = x.shape
            x_prev = jnp.concatenate([jnp.zeros((B, 1, C), x.dtype), x[:, :-1, :]], axis=1)
            xr = mu_r * x + (1.0 - mu_r) * x_prev
            xk = mu_k * x + (1.0 - mu_k) * x_prev
            r = jax.nn.sigmoid(jnp.einsum('btc,dc->btd', xr, W_r))
            k = jnp.einsum('btc,dc->btd', xk, W_k)
            k_act = jnp.square(jax.nn.relu(k))
            out = r * jnp.einsum('btc,dc->btd', k_act, W_v)
            new_state = x[:, -1, :]
            return (out, new_state)
        return _reference_tuple_inner(x, W_r, W_k, W_v, mu_r, mu_k)[0]

    def _L1_attn_ref(x, q_w, k_w, v_w, o_w):
        import math
        import jax, jax.numpy as jnp
        import numpy as np
        D_MODEL = 256
        N_HEADS = 16
        HEAD_DIM = D_MODEL // N_HEADS
        B, L = (1, 1024)

        def _slopes(n_heads):
            ratio = 2.0 ** (-8.0 / n_heads)
            return jnp.asarray([ratio ** (i + 1) for i in range(n_heads)], dtype=jnp.float32)
        b, l, _ = x.shape

        def proj(w):
            return (x @ w).reshape(b, l, N_HEADS, HEAD_DIM).transpose(0, 2, 1, 3)
        q, k, v = (proj(q_w), proj(k_w), proj(v_w))
        scale = math.sqrt(HEAD_DIM)
        scores = jnp.einsum('bhid,bhjd->bhij', q, k) / scale
        pos = jnp.arange(l)
        distance = jnp.abs(pos[None, :] - pos[:, None]).astype(jnp.float32)
        alibi = -distance[None, :, :] * _slopes(N_HEADS)[:, None, None]
        scores = scores + alibi[None]
        causal = pos[None, :] <= pos[:, None]
        scores = jnp.where(causal[None, None], scores, -jnp.inf)
        attn = jax.nn.softmax(scores, axis=-1)
        out = jnp.einsum('bhij,bhjd->bhid', attn, v)
        out = out.transpose(0, 2, 1, 3).reshape(b, l, D_MODEL)
        return out @ o_w

    def _L1_ffn_ref(x, wf, uf, bf, wi, ui, bi, wc, uc, bc, wo, uo, bo, in_c):
        import jax, jax.numpy as jnp
        import numpy as np
        from jax import lax
        T, B, I, M, O = (64, 64, 256, 256, 256)

        def _xavier(key, shape):
            fan_out, fan_in = shape
            limit = float(np.sqrt(6.0 / (fan_in + fan_out)))
            return jax.random.uniform(key, shape, jnp.float32, -limit, limit)
        batch = x.shape[1]
        c0 = jnp.broadcast_to(in_c, (batch, in_c.shape[0]))

        def step(c, xt):
            ft = jax.nn.sigmoid(xt @ wf.T + c @ uf.T + bf)
            it = jax.nn.sigmoid(xt @ wi.T + c @ ui.T + bi)
            gt = jnp.tanh(xt @ wc.T + c @ uc.T + bc)
            c = ft * c + it * gt
            return (c, None)
        c_final, _ = lax.scan(step, c0, x)
        h = jnp.tanh(jnp.einsum('tbi,oi->tbo', x, wo) + c_final @ uo.T + bo)
        return h
    x = L0_attn_x
    x = x + _L0_attn_ref(_layernorm(x, axis=-1), L0_attn_Wq, L0_attn_bq, L0_attn_Wk, L0_attn_bk, L0_attn_Wv, L0_attn_bv, L0_attn_Wo, L0_attn_bo)
    x = x + _L0_ffn_ref(_layernorm(x, axis=-1), L0_ffn_W_r, L0_ffn_W_k, L0_ffn_W_v, L0_ffn_mu_r, L0_ffn_mu_k)
    x = x + _L1_attn_ref(_layernorm(x, axis=-1), L1_attn_q_w, L1_attn_k_w, L1_attn_v_w, L1_attn_o_w)
    x = x + _L1_ffn_ref(_layernorm(x, axis=-1), L1_ffn_wf, L1_ffn_uf, L1_ffn_bf, L1_ffn_wi, L1_ffn_ui, L1_ffn_bi, L1_ffn_wc, L1_ffn_uc, L1_ffn_bc, L1_ffn_wo, L1_ffn_uo, L1_ffn_bo, L1_ffn_in_c)
    return x

_drawn_inputs = setup_inputs


def setup_inputs(seed=0):
    import zlib

    import numpy as np

    out = dict(_drawn_inputs(seed))
    spreads = {'L1_ffn_bf': (0.0, 0.744),
     'L1_ffn_bi': (0.0, 0.738),
     'L1_ffn_bc': (0.0, 0.1),
     'L1_ffn_bo': (0.0, 0.1),
     'L1_ffn_in_c': (0.0, 0.8)}
    factors = {'L0_attn_Wq': 5.42,
     'L0_attn_bq': 8.0,
     'L0_attn_Wk': 5.407,
     'L0_attn_bk': 8.0,
     'L0_ffn_W_r': 2.872,
     'L0_ffn_mu_r': 5.82}
    for name, (base, spread) in spreads.items():
        noise = np.random.default_rng([zlib.crc32(name.encode()), seed]).standard_normal(out[name].shape)
        drawn = base * np.exp(spread * noise) if base else spread * noise
        out[name] = jnp.asarray(drawn.astype(out[name].dtype))
    for name, factor in factors.items():
        out[name] = (out[name] * factor).astype(out[name].dtype)
    return out
```

```python
import concourse.bass as bass
from concourse import mybir
from contextlib import ExitStack

TERM = 16
Q_TERMS = (0, 1, 2, 0, 1, 0)
K_TERMS = (0, 0, 0, 1, 1, 2)
ROW_EXTRA = 6 * TERM
ROWS_ALIBI = 6
ROW_MAX = ROW_EXTRA + ROWS_ALIBI
ROWS = ROW_MAX + 2

W_NAMES = ("q0", "k0", "v0", "o0", "fr", "fk", "fv", "q1", "k1", "v1", "o1",
           "wf", "uf", "wi", "ui", "wc", "uc", "wo", "uo")
COL_NAMES = ("bq", "bk", "mu_r", "mu_k", "bf", "bi", "bc", "in_c")
ROW_NAMES = ("bv", "bo", "bo_rnn")

PER_TURN = dict(
    x_in=16,
    stats=16, moments=16, eps_added=4, rstd=4, normed=16,
    tr_full=12, tr_out=12,
    qk_full=8, qk_high=8, qk_rest=8, qk_mid=8, qk_low=8,
    v_full=4, v_out=4,
    parts_stored_q=32, parts_stored_k=32, stack_in=2 * 9 * 16,
    max_full=64, max_out=64,
    max_high=2, max_low=2, maxT_full=2, maxT_out=2, max_rows_in=64,
    score_full=64, exp_out=64,
    av_full=16, av_out=8,
    back_full=8, recip=8, head_out=8,
    proj_full=4, proj_out=4, bias_added=1,
    shifted_a=4, shifted=4,
    fk_full=2, relu=2, square=2, fr_full=2, gate=2, fv_full=2, gated=2, ffn_out=2,
    gates_full=6, gates_out=6, keep=1, new=1, state2=1, state=1,
    zo_full=2, zo_out=2, zo_stored=16, x_stored=16,
)

def _dense_order():
    order = []
    for layer in (0, 1):
        order += [("tr", "act")] * 2
        order += [("qk", "dve")] * 4
        order += [("v", "dve")] * 2
        order += [("maxT", "dve")]
        order += [("back", "dve")] * 4
        order += [("tr", "act")] * 2
        order += [("proj", "dve")] * 2
        order += [("tr", "act")] * 2
        if layer == 0:
            order += [("fk", "dve")] * 2 + [("fr", "act")] * 2 + [("fv", "dve")] * 2
        else:
            order += [("gates", "act")] * 6 + [("zo", "act")] * 2
    return order

DENSE = _dense_order()
FREED_BY = dict(tr="tr_out", qk="qk_rest", v="v_out", maxT="maxT_out", back="head_out",
                proj="proj_out", fk="relu", fr="gate", fv="gated", gates="gates_out", zo="zo_out")
DENSE_BANKS = 2
assert len(DENSE) % DENSE_BANKS == 0


def sequence_stack_kernel(nc, x, weights, columns, rows, ident_f, ident_b, causal, extra_q, extra_k, out):
    fp32, bf16 = mybir.dt.float32, mybir.dt.bfloat16
    ALU, ACT = mybir.AluOpType, mybir.ActivationFunctionType
    AX_X = mybir.AxisListType.X
    B, S, D = x.shape
    H, HD = 16, 16
    NT = S // 128
    NC = D // 128
    EPS = 1e-5
    SCALE = float(HD) ** -0.5

    parts_dram = [nc.dram_tensor(f"parts_{n}", (3, NC * 128, S), bf16, kind="Internal").ap()
                  for n in ("q0", "k0", "q1", "k1")]
    x_dram = nc.dram_tensor("x_after_attention", (B, S, D), fp32, kind="Internal").ap()
    zo_dram = nc.dram_tensor("output_gate_input", (B, S, D), fp32, kind="Internal").ap()

    ctx = ExitStack()
    with ctx:
        def sb(name, shape, dt=fp32):
            return ctx.enter_context(nc.sbuf_tensor(name, shape, dt))

        W = sb("W", [128, len(W_NAMES), NC, D])
        col = sb("col", [128, len(COL_NAMES), NC])
        half = sb("half", [128, 2, NC])
        one_minus = sb("one_minus", [128, 2, NC])
        row = sb("row", [128, len(ROW_NAMES), D])
        idf = sb("idf", [128, 128])
        idb = sb("idb", [128, 128], bf16)
        msk = sb("msk", [128, 128], bf16)
        zero_col = sb("zero_col", [128, 1])
        x_sb = sb("x_sb", [128, NT, D])
        xr = sb("xr", [128, NT, D])
        stat = sb("stat", [128, NT, 6])
        mom = sb("mom", [128, NT, 2])
        var_eps = sb("var_eps", [128, NT])
        minus_half = sb("minus_half", [128, NT])
        rstd = sb("rstd", [128, NT])
        eps = sb("eps", [128, NT])
        credit_cell = sb("credit_cell", [128, 8])
        gate_cell = sb("gate_cell", [128, 2])
        h_sb = sb("h_sb", [128, NT, D])
        hT = sb("hT", [128, NC, S + 1])
        rest = sb("rest", [128, 4, S])
        parts = sb("parts", [128, 2, 3, NC, S], bf16)
        Qs = [sb(f"Qs{n}", [128, H, S], bf16) for n in (0, 1)]
        Ks = sb("Ks", [128, H, S], bf16)
        V = sb("V", [128, NT, H, 32])
        mx = sb("mx", [128, NT, H])
        mparts = sb("mparts", [128, NT, 2, H], bf16)
        mT = sb("mT", [2 * H, S], bf16)
        P = sb("P", [128, 2, 4, 2 * S])
        oT = sb("oT", [128, 2, S])
        rcp = sb("rcp", [128, NT, 4])
        mix = sb("mix", [128, 2, NC, S])
        act2 = sb("act2", [128, NC, S])
        sq = sb("sq", [128, NC, S])
        gate_r = sb("gate_r", [128, NT, D])
        c2 = sb("c2", [128, NC, S])
        cT = sb("cT", [128, NC, S])

        SC = ctx.enter_context(nc.psum_tensor("SC", [128, 4, S], fp32))
        AV = ctx.enter_context(nc.psum_tensor("AV", [128, 2, S], fp32))
        DN = ctx.enter_context(nc.psum_tensor("DN", [128, DENSE_BANKS, S], fp32))

        sem = {n: ctx.enter_context(nc.semaphore(n)) for n in PER_TURN}
        for n in ("consts_in", "memsets", "minus_half_set", "halves", "state_set", "cu_full", "cu_out",
                  "z_in0", "z_in1", "zsum", "ztanh", "zfinal", "z_stored0", "z_stored1"):
            sem[n] = ctx.enter_context(nc.semaphore(n))
        def w(name):
            return W[:, W_NAMES.index(name), :, :]

        def c_(name, c):
            i = COL_NAMES.index(name)
            return col[:, i, c:c + 1]

        credited = ("x_stored", "zo_stored", "zo_out", "state", "z_stored0", "z_stored1")

        class Turn:
            def __init__(self, eng):
                self.eng, self.n, self.b = eng, {}, None

            def done(self, ins, name, by=1):
                self.n[name] = self.n.get(name, 0) + by
                ins.then_inc(sem[name], by)
                return self.n[name]

            def need(self, name, n):
                self.eng.wait_ge(sem[name], self.b * PER_TURN[name] + n + (name in credited))

            def close(self):
                for name, n in self.n.items():
                    assert n == PER_TURN[name], (name, n, PER_TURN[name])

        block = ctx.enter_context(nc.Block())

        @block.sync
        def _(sp):
            for dst, src in ((W[:], weights.rearrange("w (c p) n -> p w c n", p=128)),
                             (col[:], columns),
                             (idf[:], ident_f), (idb[:], ident_b), (msk[:], causal),
                             (Qs[0][ROW_EXTRA:ROWS], extra_q[0]), (Qs[1][ROW_EXTRA:ROWS], extra_q[1]),
                             (Ks[ROW_EXTRA:ROWS], extra_k)):
                sp.dma_start(dst, src).then_inc(sem["consts_in"], 16)
            for r in range(len(ROW_NAMES)):
                sp.dma_start(row[:, r, :], rows[r:r + 1, :].partition_broadcast(128)).then_inc(sem["consts_in"], 16)
            sp.dma_start(x_sb[:], x[0].rearrange("(t p) d -> p t d", p=128)).then_inc(sem["x_in"], 16)
            t = Turn(sp)
            with sp.Fori(0, B) as b:
                t.b = b
                for layer in (0, 1):
                    for side in (0, 1):
                        n = 4 * layer + 2 * side + 2
                        t.need("qk_low", n)
                        t.need("qk_high", n)
                        t.done(sp.dma_start(parts_dram[2 * layer + side].rearrange("t (c p) n -> p t c n", p=128),
                                            parts[:, side]), "parts_stored_" + "qk"[side], 16)
                    for side in (0, 1):
                        t.need("parts_stored_" + "qk"[side], 16 * (layer + 1))
                        src = parts_dram[2 * layer + side]
                        dst = Ks if side else Qs[layer]
                        runs = ([(k, p, 1) for k, p in enumerate(K_TERMS)] if side
                                else [(0, 0, 3), (3, 0, 2), (5, 0, 1)])
                        for k, p, m in runs:
                            t.done(sp.dma_start(dst[TERM * k:TERM * (k + m)],
                                                src[p:p + m].rearrange("t (d h) n -> (t d) h n", h=H)),
                                   "stack_in", 16)
                    t.need("maxT_out", layer + 1)
                    for part in (0, 1):
                        t.done(sp.dma_start(Qs[layer][ROW_MAX + part:ROW_MAX + part + 1], mT[H * part:H * (part + 1), :]),
                               "max_rows_in", 16)
                    if layer == 0:
                        t.need("proj_out", 2)
                        t.done(sp.dma_start(x_sb[:], x[bass.ds(sp.snap((b + 1) % B), 1)]
                                            .rearrange("o (t p) d -> p (o t) d", p=128)), "x_in", 16)
                t.need("proj_out", 4)
                t.done(sp.dma_start(x_dram[bass.ds(b, 1)].rearrange("o (t p) d -> p (o t) d", p=128), xr[:]), "x_stored", 16)
                t.need("zo_out", 2)
                t.done(sp.dma_start(zo_dram[bass.ds(b, 1)].rearrange("o (t p) d -> p (o t) d", p=128), gate_r[:]), "zo_stored", 16)
            t.close()
            sp.wait_ge(sem["x_stored"], 16 * B + 1)
            sp.wait_ge(sem["zo_stored"], 16 * B + 1)
            sp.wait_ge(sem["x_in"], 16 * (B + 1))
            sp.wait_ge(sem["cu_out"], 2)
            with sp.Fori(0, B // 2) as i:
                for p in (0, 1):
                    sp.wait_ge(sem[f"z_stored{p}"], 16 * i + 1)
                    n = sp.snap(2 * i + p)
                    sp.dma_start(mix[:, p].rearrange("p c n -> p (c n)").rearrange("p (t d) -> p t d", d=D),
                                 zo_dram[bass.ds(n, 1)].rearrange("o (t p) d -> p (o t) d", p=128))\
                      .then_inc(sem[f"z_in{p}"], 16)
                    sp.dma_start((x_sb, xr)[p][:],
                                 x_dram[bass.ds(n, 1)].rearrange("o (t p) d -> p (o t) d", p=128))\
                      .then_inc(sem[f"z_in{p}"], 16)
                for p in (0, 1):
                    sp.wait_ge(sem["zfinal"], 2 * i + p + 1)
                    sp.dma_start(out[bass.ds(sp.snap(2 * i + p), 1)].rearrange("o (t p) d -> p (o t) d", p=128),
                                 (x_sb, xr)[p][:]).then_inc(sem[f"z_stored{p}"], 16)
            for p in (0, 1):
                sp.wait_ge(sem[f"z_stored{p}"], 16 * (B // 2) + 1)

        def z_pair(p):
            return mix[:, p].rearrange("p c n -> p (c n)")

        @block.gpsimd
        def _(pool):
            pool.wait_ge(sem["memsets"], N_MEMSETS)
            pool.wait_ge(sem["consts_in"], CONSTS)
            t = Turn(pool)
            norm_no = [0]

            def rstd_of_rows():
                n = norm_no[0] = norm_no[0] + 1
                t.need("moments", 4 * n)
                pos = t.done(pool.tensor_tensor(var_eps[:], mom[:, :, 1], eps[:], ALU.add), "eps_added")
                t.need("eps_added", pos)
                t.done(pool.tensor_tensor(rstd[:], var_eps[:], minus_half[:], ALU.pow), "rstd")

            with pool.Fori(0, B) as b:
                t.b = b
                for layer in (0, 1):
                    rstd_of_rows()
                    if layer == 0:
                        t.need("normed", 4)
                        for tt in range(NT):
                            ins = pool.tensor_tensor(x_sb[:, tt, :], x_sb[:, tt, :], row[:, 1, :], ALU.add)
                        t.done(ins, "bias_added")
                    for k in range(4):
                        side, c = k // 2, k % 2
                        t.need("qk_rest", 4 * layer + k + 1)
                        pool.tensor_tensor(gate_cell[:, 0:1], minus_half[:, 0:1], minus_half[:, 0:1], ALU.add)
                        pos = t.done(pool.tensor_copy(parts[:, side, 1, c, :], rest[:, k, :]), "qk_mid")
                        t.need("qk_mid", pos)
                        t.done(pool.tensor_tensor(parts[:, side, 2, c, :], rest[:, k, :], parts[:, side, 1, c, :],
                                                  ALU.subtract), "qk_low")
                    rstd_of_rows()
                    if layer == 0:
                        for c in range(NC):
                            t.need("relu", c + 1)
                            t.done(pool.tensor_tensor(sq[:, c, :], act2[:, c, :], act2[:, c, :], ALU.mult), "square")
            t.close()
            pool.wait_ge(sem["cu_out"], 2)
            with pool.Fori(0, B // 2) as i:
                for p in (0, 1):
                    pool.wait_ge(sem[f"z_in{p}"], 32 * i + 32)
                    pool.tensor_tensor(z_pair(p), z_pair(p), h_sb[:].rearrange("p t d -> p (t d)"), ALU.add)\
                        .then_inc(sem["zsum"], 1)

        @block.scalar
        def _(act):
            act.wait_ge(sem["memsets"], N_MEMSETS)
            act.wait_ge(sem["consts_in"], CONSTS)
            act.wait_ge(sem["halves"], 4)
            t = Turn(act)
            slot = iter(())

            def transposed(n):
                for c in range(NC):
                    k = next(slot)
                    t.need("tr_full", 2 * n + c + 1)
                    t.done(act.activation(hT[:, c, 1:S + 1], DN[:, k % DENSE_BANKS, :], ACT.Copy), "tr_out")

            def skip(kind, n):
                for _ in range(n):
                    assert DENSE[next(slot)][0] == kind

            with act.Fori(0, B) as b:
                t.b = b
                slot = iter(range(len(DENSE)))
                for layer in (0, 1):
                    transposed(3 * layer)
                    for k in range(4):
                        side, c = k // 2, k % 2
                        d = next(slot)
                        t.need("qk_full", 4 * layer + k + 1)
                        bias = c_(("bq", "bk")[side], c) if layer == 0 else zero_col[:]
                        t.done(act.activation(parts[:, side, 0, c, :], DN[:, d % DENSE_BANKS, :], ACT.Identity,
                                              bias=bias), "qk_high")
                    skip("v", 2)
                    skip("maxT", 1)
                    skip("back", 4)
                    for u in range(32):
                        blk, j = u // 4, u % 4
                        if blk >= 2 and j == 0:
                            t.need("av_full", 8 * layer + blk - 1)
                        t.need("score_full", 32 * layer + u + 1)
                        n = exp_columns(layer, blk % 2)
                        src = SC[:, 2 * (u % 2):2 * (u % 2) + 2, :].rearrange("p a n -> p (a n)")[:, 0:n]
                        t.done(act.activation(P[:, blk % 2, j, 0:n], src, ACT.Exp, scale=SCALE), "exp_out")
                    transposed(3 * layer + 1)
                    skip("proj", 2)
                    transposed(3 * layer + 2)
                    if layer == 0:
                        skip("fk", 2)
                        t.need("zo_stored", 0)
                        for i in range(2):
                            d = next(slot)
                            t.need("fr_full", i + 1)
                            t.done(act.activation(gate_r[:, 2 * i:2 * i + 2, :].rearrange("p t d -> p (t d)"),
                                                  DN[:, d % DENSE_BANKS, :], ACT.Tanh, scale=0.5), "gate")
                        skip("fv", 2)
                    else:
                        for k in range(6):
                            gate, c = k // 2, k % 2
                            d = next(slot)
                            t.need("gates_full", k + 1)
                            dst, bias, scale = ((mix[:, 0, c, :], half[:, 0, c:c + 1], 0.5),
                                                (mix[:, 1, c, :], half[:, 1, c:c + 1], 0.5),
                                                (act2[:, c, :], c_("bc", c), 1.0))[gate]
                            t.done(act.activation(dst, DN[:, d % DENSE_BANKS, :], ACT.Tanh, bias=bias, scale=scale),
                                   "gates_out")
                        for i in range(2):
                            d = next(slot)
                            t.need("zo_full", i + 1)
                            t.done(act.activation(gate_r[:, 2 * i:2 * i + 2, :].rearrange("p t d -> p (t d)"),
                                                  DN[:, d % DENSE_BANKS, :], ACT.Copy), "zo_out")
            t.close()
            with act.Fori(0, B // 2) as i:
                for p in (0, 1):
                    act.wait_ge(sem["zsum"], 2 * i + p + 1)
                    act.activation(z_pair(p), z_pair(p), ACT.Tanh).then_inc(sem["ztanh"], 1)

        @block.vector
        def _(dve):
            for buf, value in ((hT[:, :, 0:1], 0.0), (zero_col[:], 0.0), (V[:, :, :, HD:32], 1.0),
                               (minus_half[:], -0.5), (c2[:], 0.0), (eps[:], EPS)):
                dve.memset(buf, value).then_inc(sem["memsets"], 1)
            for i, n in enumerate(credited):
                dve.memset(credit_cell[:, i:i + 1], 0.0).then_inc(sem[n], 1)
            dve.wait_ge(sem["memsets"], N_MEMSETS)
            dve.wait_ge(sem["consts_in"], CONSTS)
            i_mu, i_f = COL_NAMES.index("mu_r"), COL_NAMES.index("bf")
            dve.tensor_scalar(one_minus[:], col[:, i_mu:i_mu + 2, :], -1.0, 1.0, ALU.mult, ALU.add).then_inc(sem["halves"], 1)
            dve.tensor_scalar(half[:], col[:, i_f:i_f + 2, :], 0.5, None, ALU.mult).then_inc(sem["halves"], 1)
            for c in range(NC):
                dve.tensor_scalar(cT[:, c, :], c2[:, c, :], c_("in_c", c), None, ALU.add).then_inc(sem["halves"], 1)
            dve.wait_ge(sem["halves"], 4)
            dve.tensor_scalar(c2[:], cT[:], 2.0, None, ALU.mult).then_inc(sem["state_set"], 1)
            dve.wait_ge(sem["state_set"], 1)
            t = Turn(dve)
            slot = iter(())
            no = dict(norm=0)

            def skip(kind, n):
                for _ in range(n):
                    assert DENSE[next(slot)][0] == kind

            def norm(src):
                n = no["norm"]
                no["norm"] += 1
                for tt in range(NT):
                    t.done(dve.bn_stats(stat[:, tt, :], src[:, tt, :]), "stats")
                t.need("stats", 4 * n + 4)
                dve.memset(gate_cell[:, 1:2], 0.0)
                for tt in range(NT):
                    t.done(dve.bn_aggr(mom[:, tt, :], stat[:, tt, :]), "moments")
                t.need("rstd", n + 1)
                for tt in range(NT):
                    t.done(dve.tensor_scalar(h_sb[:, tt, :], src[:, tt, :], mom[:, tt, 0:1], rstd[:, tt:tt + 1],
                                             ALU.subtract, ALU.mult), "normed")

            with dve.Fori(0, B) as b:
                t.b = b
                slot = iter(range(len(DENSE)))
                for layer in (0, 1):
                    if layer == 0:
                        t.need("x_in", 16)
                    norm(x_sb if layer == 0 else xr)
                    skip("tr", 2)
                    for k in range(4):
                        side, c = k // 2, k % 2
                        d = next(slot)
                        t.need("qk_high", 4 * layer + k + 1)
                        bias = c_(("bq", "bk")[side], c) if layer == 0 else zero_col[:]
                        t.done(dve.scalar_tensor_tensor(rest[:, k, :], DN[:, d % DENSE_BANKS, :], bias,
                                                        parts[:, side, 0, c, :], ALU.add, ALU.subtract), "qk_rest")
                    for i in range(2):
                        d = next(slot)
                        t.need("v_full", 2 * layer + i + 1)
                        for a in (0, 1):
                            dst = V[:, 2 * i + a, :, 0:HD]
                            src = DN[:, d % DENSE_BANKS, a * D:(a + 1) * D].rearrange("p (h d) -> p h d", d=HD)
                            if layer == 0:
                                ins = dve.tensor_tensor(dst, src, row[:, 0, :].rearrange("p (h d) -> p h d", d=HD), ALU.add)
                            else:
                                ins = dve.tensor_copy(dst, src)
                        t.done(ins, "v_out")
                    for u in range(32):
                        qt, pair = u // 8, u % 8
                        t.need("max_full", 32 * layer + u + 1)
                        keys = S if layer == 0 else 128 * (qt + 1)
                        t.done(dve.reduce_max(mx[:, qt, 2 * pair:2 * pair + 2],
                                              SC[:, 2 * (u % 2):2 * (u % 2) + 2, 0:keys], axis=AX_X), "max_out")
                    t.need("max_out", 32 * (layer + 1))
                    t.done(dve.tensor_scalar(mparts[:, :, 0, :], mx[:], -1.0, None, ALU.mult), "max_high")
                    t.need("max_high", layer + 1)
                    t.done(dve.scalar_tensor_tensor(mparts[:, :, 1, :], mx[:], -1.0, mparts[:, :, 0, :],
                                                    ALU.mult, ALU.subtract), "max_low")
                    d = next(slot)
                    t.need("maxT_full", layer + 1)
                    t.done(dve.tensor_copy(mT[:], DN[0:2 * H, d % DENSE_BANKS, :].bitcast(bf16)[:, 0:S]), "maxT_out")

                    def unload(g):
                        t.need("av_full", 8 * layer + 2 * g + 2)
                        if g >= 2:
                            t.need("back_full", 4 * layer + g - 1)
                        t.done(dve.tensor_copy(oT[:, g % 2, :], AV[:, g % 2, :]), "av_out")

                    def normalise(g):
                        d = next(slot)
                        t.need("back_full", 4 * layer + g + 1)
                        back = DN[:, d % DENSE_BANKS, :].rearrange("p (t h m) -> p t h m", h=4, m=32)
                        pos = t.done(dve.reciprocal(rcp[:], back[:, :, :, HD]), "recip")
                        t.need("recip", pos)
                        t.done(dve.tensor_tensor(
                            h_sb[:, :, 4 * HD * g:4 * HD * (g + 1)].rearrange("p t (h d) -> p t h d", d=HD),
                            back[:, :, :, 0:HD], rcp[:].unsqueeze(3).to_broadcast([128, NT, 4, HD]), ALU.mult), "head_out")

                    for g in range(4):
                        unload(g)
                        normalise(g)
                    skip("tr", 2)
                    if layer == 0:
                        t.need("bias_added", 1)
                        t.need("x_stored", 0)
                    for i in range(2):
                        d = next(slot)
                        t.need("proj_full", 2 * layer + i + 1)
                        src = x_sb if layer == 0 else xr
                        both = slice(2 * i, 2 * i + 2)
                        t.done(dve.tensor_tensor(xr[:, both, :], DN[:, d % DENSE_BANKS, :].rearrange("p (t d) -> p t d", d=D),
                                                 src[:, both, :], ALU.add), "proj_out")
                    t.need("proj_out", 2 * layer + 2)
                    norm(xr)
                    skip("tr", 2)
                    if layer == 0:
                        t.need("tr_out", 6)
                        for m in (0, 1):
                            for c in range(NC):
                                t.done(dve.tensor_scalar(mix[:, m, c, :], hT[:, c, 1:S + 1],
                                                         c_(("mu_r", "mu_k")[m], c), None, ALU.mult), "shifted_a")
                        for m in (0, 1):
                            for c in range(NC):
                                t.need("shifted_a", 2 * m + c + 1)
                                t.done(dve.scalar_tensor_tensor(mix[:, m, c, :], hT[:, c, 0:S], one_minus[:, m, c:c + 1],
                                                                mix[:, m, c, :], ALU.mult, ALU.add), "shifted")
                        for c in range(NC):
                            d = next(slot)
                            t.need("fk_full", c + 1)
                            t.done(dve.tensor_scalar(act2[:, c, :], DN[:, d % DENSE_BANKS, :], 0.0, None, ALU.max), "relu")
                        skip("fr", 2)
                        for i in range(2):
                            d = next(slot)
                            both = slice(2 * i, 2 * i + 2)
                            t.need("fv_full", i + 1)
                            t.need("gate", i + 1)
                            t.done(dve.scalar_tensor_tensor(h_sb[:, both, :], gate_r[:, both, :], 1.0,
                                                            DN[:, d % DENSE_BANKS, :].rearrange("p (t d) -> p t d", d=D),
                                                            ALU.add, ALU.mult), "gated")
                            t.need("gated", i + 1)
                            t.done(dve.scalar_tensor_tensor(xr[:, both, :], h_sb[:, both, :], 0.5, xr[:, both, :],
                                                            ALU.mult, ALU.add), "ffn_out")
                        t.need("ffn_out", 2)
                    else:
                        skip("gates", 6)
                        t.need("gates_out", 4)
                        t.done(dve.scalar_tensor_tensor(c2[:], mix[:, 0], 1.0, c2[:], ALU.add, ALU.mult), "keep")
                        t.need("gates_out", 6)
                        t.done(dve.scalar_tensor_tensor(act2[:], mix[:, 1], 1.0, act2[:], ALU.add, ALU.mult), "new")
                        t.need("new", 1)
                        t.need("keep", 1)
                        t.done(dve.scalar_tensor_tensor(c2[:], c2[:], 0.5, act2[:], ALU.mult, ALU.add), "state2")
                        t.need("state2", 1)
                        t.done(dve.tensor_scalar(cT[:], c2[:], 0.5, None, ALU.mult), "state")
                        skip("zo", 2)
            t.close()
            for i in range(2):
                dve.wait_ge(sem["cu_full"], i + 1)
                for a in (0, 1):
                    ins = dve.tensor_tensor(h_sb[:, 2 * i + a, :], DN[:, i, a * D:(a + 1) * D], row[:, 2, :], ALU.add)
                ins.then_inc(sem["cu_out"], 1)
            with dve.Fori(0, B // 2) as i:
                for p in (0, 1):
                    dve.wait_ge(sem["ztanh"], 2 * i + p + 1)
                    dst = (x_sb, xr)[p][:].rearrange("p t d -> p (t d)")
                    dve.tensor_tensor(dst, dst, z_pair(p), ALU.add).then_inc(sem["zfinal"], 1)

        @block.tensor
        def _(pe):
            pe.wait_ge(sem["memsets"], N_MEMSETS)
            pe.wait_ge(sem["consts_in"], CONSTS)
            pe.wait_ge(sem["state_set"], 1)
            t = Turn(pe)
            used = []
            seen = {}

            def bank(kind):
                s = len(used)
                assert DENSE[s][0] == kind
                used.append(kind)
                if s >= DENSE_BANKS:
                    old = DENSE[s - DENSE_BANKS][0]
                    t.need(FREED_BY[old], sum(k[0] == old for k in DENSE[:s - DENSE_BANKS + 1]))
                else:
                    t.need("zo_out", 0)
                return DN[:, s % DENSE_BANKS, :]

            def transposes(name, n):
                for c in range(NC):
                    o = bank("tr")
                    for tt in range(NT):
                        if name == "normed":
                            t.need("normed", n + tt + 1)
                        elif tt == 0:
                            t.need("head_out", n + 2 * c + 2)
                        ins = pe.transpose(o[:, 128 * tt:128 * tt + 128], h_sb[:, tt, 128 * c:128 * c + 128], idf[:])
                    t.done(ins, "tr_full")

            def features(kind, name, rhs):
                for c in range(NC):
                    o = bank(kind)
                    for kc in range(NC):
                        ins = pe.matmul(o, w(name)[:, kc, 128 * c:128 * c + 128], rhs(kc), start=kc == 0, stop=kc == NC - 1)
                    t.done(ins, kind + "_full")

            def tokens(kind, name, lhs, before=None):
                for i in range(2):
                    o = bank(kind)
                    if before:
                        before(i)
                    for a in (0, 1):
                        for kc in range(NC):
                            ins = pe.matmul(o[:, a * D:(a + 1) * D], lhs(kc, 2 * i + a), w(name)[:, kc, :],
                                            start=kc == 0, stop=kc == NC - 1)
                    t.done(ins, kind + "_full")

            def hT_tile(kc, tt):
                return hT[:, kc, 1 + 128 * tt:1 + 128 * tt + 128]

            with pe.Fori(0, B) as b:
                t.b = b
                used.clear()
                for layer in (0, 1):
                    L = "01"[layer]
                    transposes("normed", 8 * layer)
                    t.need("tr_out", 6 * layer + 2)
                    for name in ("q" + L, "k" + L):
                        features("qk", name, lambda kc: hT[:, kc, 1:S + 1])
                    tokens("v", "v" + L, hT_tile)
                    t.need("stack_in", 144 * (layer + 1))
                    for u in range(32):
                        qt, pair = u // 8, u % 8
                        if u >= 2:
                            t.need("max_out", 32 * layer + u - 1)
                        keys = S if layer == 0 else 128 * (qt + 1)
                        for a in (0, 1):
                            h = 2 * pair + a
                            o = SC[:, 2 * (u % 2) + a, :]
                            ins = pe.matmul(o[:, 0:keys], Qs[layer][0:(ROW_EXTRA, ROW_MAX)[layer], h, 128 * qt:128 * qt + 128],
                                            Ks[0:(ROW_EXTRA, ROW_MAX)[layer], h, 0:keys], start=True, stop=layer == 0)
                            if layer == 1:
                                ins = pe.matmul(o[:, keys - 128:keys], idb[:], msk[:], start=False, stop=True)
                        t.done(ins, "max_full")
                    o = bank("maxT")
                    t.need("max_low", layer + 1)
                    for tt in range(NT):
                        ins = pe.transpose(o[0:2 * H, :].bitcast(bf16)[:, 128 * tt:128 * tt + 128],
                                           mparts[:, tt].rearrange("p a h -> p (a h)"), idb[:])
                    t.done(ins, "maxT_full")
                    t.need("max_rows_in", 32 * (layer + 1))

                    def scores(blk, j):
                        u = 4 * blk + j
                        h, pair = 4 * (blk // 2) + j, blk % 2
                        if u >= 2:
                            t.need("exp_out", 32 * layer + u - 1)
                        flat = SC[:, 2 * (u % 2):2 * (u % 2) + 2, :].rearrange("p a n -> p (a n)")
                        for kt, q0, at, n in key_tiles(layer, pair):
                            ins = pe.matmul(flat[:, at:at + n], Ks[0:ROWS, h, 128 * kt:128 * kt + 128],
                                            Qs[layer][0:ROWS, h, q0:S], start=True, stop=layer == 0)
                            if layer == 1:
                                ins = pe.matmul(flat[:, at:at + 128], msk[:], idb[:], start=False, stop=True)
                        t.done(ins, "score_full")

                    def with_values(blk):
                        g, pair = blk // 2, blk % 2
                        t.need("exp_out", 32 * layer + 4 * blk + 4)
                        if g >= 2 and pair == 0:
                            t.need("av_out", 4 * layer + g - 1)
                        for kt, q0, at, n in key_tiles(layer, pair):
                            for j in range(4):
                                ins = pe.matmul(AV[32 * j:32 * j + 32, g % 2, q0:S], V[:, kt, 4 * g + j, :],
                                                P[:, blk % 2, j, at:at + n], start=kt == 0, stop=kt == NT - 1)
                        t.done(ins, "av_full")

                    def back(g):
                        o = bank("back")
                        t.need("av_out", 4 * layer + g + 1)
                        for tt in range(NT):
                            ins = pe.transpose(o[:, 128 * tt:128 * tt + 128], oT[:, g % 2, 128 * tt:128 * tt + 128], idf[:])
                        t.done(ins, "back_full")

                    for blk in range(8):
                        for j in range(4):
                            scores(blk, j)
                        if blk:
                            with_values(blk - 1)
                        if blk >= 3 and blk % 2:
                            back((blk - 3) // 2)
                    with_values(7)
                    back(3)
                    transposes("head_out", 4 * layer)
                    t.need("tr_out", 6 * layer + 4)
                    tokens("proj", "o" + L, hT_tile)
                    transposes("normed", 8 * layer + 4)
                    t.need("tr_out", 6 * layer + 6)
                    if layer == 0:
                        t.need("shifted", 4)
                        features("fk", "fk", lambda kc: mix[:, 1, kc, :])
                        tokens("fr", "fr", lambda kc, tt: mix[:, 0, kc, 128 * tt:128 * tt + 128])
                        t.need("square", 2)
                        tokens("fv", "fv", lambda kc, tt: sq[:, kc, 128 * tt:128 * tt + 128])
                    else:
                        t.need("state", 0)
                        for gate in "fic":
                            for c in range(NC):
                                o = bank("gates")
                                for kc in range(NC):
                                    pe.matmul(o, w("w" + gate)[:, kc, 128 * c:128 * c + 128], hT[:, kc, 1:S + 1],
                                              start=kc == 0, stop=False)
                                for kc in range(NC):
                                    ins = pe.matmul(o, w("u" + gate)[:, kc, 128 * c:128 * c + 128], cT[:, kc, :],
                                                    start=False, stop=kc == NC - 1)
                                t.done(ins, "gates_full")
                        tokens("zo", "wo", hT_tile)
            t.close()
            pe.wait_ge(sem["state"], B + 1)
            pe.wait_ge(sem["zo_out"], 2 * B + 1)
            for i in range(2):
                for a in (0, 1):
                    for kc in range(NC):
                        ins = pe.matmul(DN[:, i, a * D:(a + 1) * D], cT[:, kc, 128 * (2 * i + a):128 * (2 * i + a) + 128],
                                        w("uo")[:, kc, :], start=kc == 0, stop=kc == NC - 1)
                ins.then_inc(sem["cu_full"], 1)


N_MEMSETS = 6
CONSTS = 16 * 11


def key_tiles(layer, pair):
    found, at = [], 0
    for kt in (2 * pair, 2 * pair + 1):
        q0 = 128 * kt if layer else 0
        found.append((kt, q0, at, 512 - q0))
        at += 512 - q0
    return found


def exp_columns(layer, pair):
    return sum(n for *_, n in key_tiles(layer, pair))


def _split(a, dtype):
    import numpy as np
    parts = []
    for _ in range(3):
        p = a.astype(dtype)
        parts.append(p)
        a = a - p.astype(np.float64)
    return parts


def _constants():
    import numpy as np
    bf = mybir.dt.np(mybir.dt.bfloat16)
    H, S = 16, 512
    ratio = 2.0 ** (-8.0 / H)
    slopes = np.array([ratio ** (i + 1) for i in range(H)], np.float32).astype(np.float64)
    line = 4.0 * slopes[:, None] * np.arange(S)[None, :]
    n = ROWS - ROW_EXTRA
    q = np.zeros((2, n, H, S), bf)
    k = np.zeros((n, H, S), bf)
    for i, (kp, qp) in enumerate(zip(_split(line, bf), _split(-line, bf))):
        q[1, i], k[i] = 1.0, kp
        q[1, 3 + i], k[3 + i] = qp, 1.0
    k[ROWS_ALIBI:] = 1.0
    causal = np.where(np.arange(128)[None, :] > np.arange(128)[:, None], -1e30, 0.0).astype(bf)
    return dict(ident_f=np.eye(128, dtype=np.float32), ident_b=np.eye(128).astype(bf), causal=causal,
                extra_q=q, extra_k=k)


def kernel(**inputs):
    import numpy as np
    import concourse.bacc as bacc
    from concourse.bass_utils import run_bass_kernel_spmd

    a = {n: np.asarray(v) for n, v in inputs.items()}
    d_major = np.arange(256).reshape(16, 16).T.reshape(-1)
    weights = np.stack([
        a["L0_attn_Wq"][:, d_major], a["L0_attn_Wk"][:, d_major], a["L0_attn_Wv"], a["L0_attn_Wo"],
        a["L0_ffn_W_r"].T, a["L0_ffn_W_k"].T, a["L0_ffn_W_v"].T,
        a["L1_attn_q_w"][:, d_major], a["L1_attn_k_w"][:, d_major], a["L1_attn_v_w"], a["L1_attn_o_w"],
        a["L1_ffn_wf"].T, a["L1_ffn_uf"].T, a["L1_ffn_wi"].T, a["L1_ffn_ui"].T,
        a["L1_ffn_wc"].T, a["L1_ffn_uc"].T, a["L1_ffn_wo"].T, a["L1_ffn_uo"].T])
    columns = np.stack([a["L0_attn_bq"][d_major], a["L0_attn_bk"][d_major], a["L0_ffn_mu_r"], a["L0_ffn_mu_k"],
                        a["L1_ffn_bf"], a["L1_ffn_bi"], a["L1_ffn_bc"], a["L1_ffn_in_c"]])
    columns = columns.reshape(len(COL_NAMES), 2, 128).transpose(2, 0, 1)
    rows = np.stack([a["L0_attn_bv"], a["L0_attn_bo"], a["L1_ffn_bo"]])
    arrays = dict(x=a["L0_attn_x"], weights=weights, columns=columns, rows=rows, **_constants())
    arrays = {n: np.ascontiguousarray(v) for n, v in arrays.items()}

    nc = bacc.Bacc("TRN2", target_bir_lowering=False, num_devices=1)
    args = [nc.dram_tensor(n, v.shape, mybir.dt.from_np(v.dtype), kind="ExternalInput").ap()
            for n, v in arrays.items()]
    out = nc.dram_tensor("out", arrays["x"].shape, mybir.dt.float32, kind="ExternalOutput").ap()
    sequence_stack_kernel(nc, *args, out)
    result = run_bass_kernel_spmd(nc, [arrays], core_ids=[0])
    return result.results[0]["out"]
```

```python
import concourse.bass as bass
from concourse import mybir
from contextlib import ExitStack

TERM = 16
Q_TERMS = (0, 1, 2, 0, 1, 0)
K_TERMS = (0, 0, 0, 1, 1, 2)
ROW_EXTRA = 6 * TERM
ROWS_ALIBI = 6
ROW_MAX = ROW_EXTRA + ROWS_ALIBI
ROWS = ROW_MAX + 2

W_NAMES = ("q0", "k0", "v0", "o0", "fr", "fk", "fv", "q1", "k1", "v1", "o1",
           "wf", "uf", "wi", "ui", "wc", "uc", "wo", "uo")
COL_NAMES = ("bq", "bk", "mu_r", "mu_k", "bf", "bi", "bc", "in_c")
ROW_NAMES = ("bv", "bo", "bo_rnn")


BEATS = 32
LOOP_START = 2
B_TOTAL = 16
DENSE_BANKS = 3


def _steps():
    table = [[[] for _ in range(BEATS)] for _ in (0, 1)]

    def put(slot, beat, kind, layer, off, index=0):
        table[slot][beat].append((kind, layer, off, index))

    for slot in (0, 1):
        e_layer, e_off, m_layer, m_off = SLOTS[slot]
        p_layer, p_off, pm_layer, pm_off = SLOTS[1 - slot]
        before = 0 if slot else -1
        put(slot, 2, "back", p_layer, p_off + before, 3)
        for g in range(3):
            put(slot, 8 * g + 10, "back", e_layer, e_off, g)
        put(slot, 0, "maxT", pm_layer, pm_off + before, 1)
        put(slot, 18, "maxT", m_layer, m_off, 0)
    for k in (0, 1):
        put(0, k, "v", 1, -1, k)
        put(0, 3 + k, "onT", 1, -2, k)
        put(0, 5 + k, "proj", 1, -2, k)
    put(0, 6, "norm4", 1, -2)
    put(0, 7, "unit4", 1, -2)
    for k in (0, 1):
        put(0, 9 + k, "nT4", 1, -2, k)
    for k in range(6):
        put(0, 11 + k, "gates", 1, -2, k)
    put(0, 13, "norm1", 0, 1)
    put(0, 14, "unit1", 0, 1)
    put(0, 16, "recur", 1, -2)
    for k in (0, 1):
        put(0, 17 + k, "zo", 1, -2, k)
        put(0, 19 + k, "nT1", 0, 1, k)
    for k in range(4):
        put(0, 21 + k, "qk", 0, 1, k)
    for k in (0, 1):
        put(1, k, "v", 0, 1, k)
        put(1, 3 + k, "onT", 0, 0, k)
        put(1, 5 + k, "proj", 0, 0, k)
    put(1, 6, "norm2", 0, 0)
    put(1, 7, "unit2", 0, 0)
    for k in (0, 1):
        put(1, 9 + k, "nT2", 0, 0, k)
    put(1, 10, "mix", 0, 0)
    for k in (0, 1):
        put(1, 12 + k, "fk", 0, 0, k)
        put(1, 14 + k, "fr", 0, 0, k)
        put(1, 16 + k, "fv", 0, 0, k)
    put(1, 17, "norm3", 0, 0)
    put(1, 18, "unit3", 0, 0)
    for k in (0, 1):
        put(1, 20 + k, "nT3", 0, 0, k)
    for k in range(4):
        put(1, 22 + k, "qk", 1, 0, k)
    return table


SLOTS = ((0, 0, 1, -1), (1, -1, 0, 1))
BANKED = ("v", "onT", "proj", "nT1", "nT2", "nT3", "nT4", "gates", "zo", "qk", "fk", "fr", "fv", "back", "maxT")
STEPS = _steps()
ORDER = [s for slot in STEPS for beat in slot for s in beat if s[0] in BANKED]
PLACE = {s: n for n, s in enumerate(ORDER)}
assert len(PLACE) == len(ORDER)
IN_TURN = -(-len(ORDER) // DENSE_BANKS) * DENSE_BANKS
ORDER += [None] * (IN_TURN - len(ORDER))

OTHER_EXP = (-2, 1)
OTHER_MAX = (-2, 1)

MAX_START = (3, 0)


def max_units(slot, beat):
    start = MAX_START[slot]
    edge = lambda t: max(0, t - start) * 32 // (BEATS - start)
    units = range(edge(beat), edge(beat + 1))
    return units[:len(units) - len(units) // 2], units[len(units) - len(units) // 2:]


PER_SEQ = dict(x_in=16, res_in=16, bias_added=1, x2_stored=16, x2_in=16, x3_stored=16, zo_stored=16,
               shifted_a=4, shifted=4, square=2, ffn_out=2, keep=1, new=1, state=1)
for _n in "1234":
    PER_SEQ.update({"stats" + _n: 4, "moments" + _n: 4, "eps" + _n: 1, "rstd" + _n: 1, "normed" + _n: 4,
                    f"nT{_n}_full": 2, f"nT{_n}_out": 2})
for _l in "01":
    PER_SEQ.update({k + _l: n for k, n in dict(
        v_full=2, v_out=2, onT_full=2, onT_out=2, proj_full=2, proj_out=2, qk_full=4, qk_high=4, qk_out=4,
        qk_mid=4, qk_low=4, back_full=4, recip=4, back_out=4, maxT_full=2, maxT_out=2, max_high=2, max_low=2,
        max_full=32, max_out=32, score_full=32, exp_out=32, av_full=16, av_out=4,
        q_stored=16, k_stored=16, stack_lo=144, stack_hi=144, rows_lo=32, rows_hi=32).items()})
PER_SEQ.update(gates_full1=6, gates_out1=6, zo_full1=2, zo_out1=2, fk_full0=2, fk_out0=2, fr_full0=2, fr_out0=2,
               fv_full0=2, fv_out0=2)


def freed_by(step):
    kind, layer, _, index = step
    name = kind + "_out" if kind[0] == "n" else f"{kind}_out{layer}"
    return name, index + 1


def sequence_stack_kernel(nc, x, weights, columns, rows, ident_f, ident_b, causal, extra_q, extra_k, out):
    fp32, bf16 = mybir.dt.float32, mybir.dt.bfloat16
    ALU, ACT = mybir.AluOpType, mybir.ActivationFunctionType
    AX_X = mybir.AxisListType.X
    B, S, D = x.shape
    assert B == B_TOTAL
    H, HD = 16, 16
    NT = S // 128
    NC = D // 128
    EPS = 1e-5
    SCALE = float(HD) ** -0.5

    parts_dram = [[nc.dram_tensor(f"parts_{n}{layer}", (3, NC * 128, S), bf16, kind="Internal").ap() for n in "qk"]
                  for layer in (0, 1)]
    x2_dram = nc.dram_tensor("x_after_layer0", (B, S, D), fp32, kind="Internal").ap()
    x3_dram = nc.dram_tensor("x_after_attention1", (B, S, D), fp32, kind="Internal").ap()
    zo_dram = nc.dram_tensor("output_gate_input", (B, S, D), fp32, kind="Internal").ap()

    ctx = ExitStack()
    with ctx:
        def sb(name, shape, dt=fp32):
            return ctx.enter_context(nc.sbuf_tensor(name, shape, dt))

        W = sb("W", [128, len(W_NAMES), NC, D])
        col = sb("col", [128, len(COL_NAMES), NC])
        half = sb("half", [128, 2, NC])
        one_minus = sb("one_minus", [128, 2, NC])
        row = sb("row", [128, len(ROW_NAMES), D])
        idf = sb("idf", [128, 128])
        idb = sb("idb", [128, 128], bf16)
        msk = sb("msk", [128, 128], bf16)
        zero_col = sb("zero_col", [128, 1])
        x_sb = sb("x_sb", [128, NT, D])
        xres = [sb("xres0", [128, NT, D]), sb("xres1", [128, NT, D])]
        stat = sb("stat", [128, NT, 6])
        mom = sb("mom", [128, NT, 2])
        var_eps = sb("var_eps", [128, NT])
        minus_half = sb("minus_half", [128, NT])
        rstd = sb("rstd", [128, NT])
        eps = sb("eps", [128, NT])
        credit_cell = sb("credit_cell", [128, 4])
        wait_cell = sb("wait_cell", [128, 2])
        h_sb = sb("h_sb", [128, NT, D])
        on = [sb("on0", [128, NT, D]), sb("on1", [128, NT, D])]
        hT = sb("hT", [128, NC, S + 1])
        rest = sb("rest", [128, 2, S])
        parts = sb("parts", [128, 2, 3, NC, S], bf16)
        Qs = [sb(f"Qs{n}", [128, H, S], bf16) for n in (0, 1)]
        Ks = [sb(f"Ks{n}", [128, H, S], bf16) for n in (0, 1)]
        V = [sb(f"V{n}", [128, NT, H, 32]) for n in (0, 1)]
        mx = [sb(f"mx{n}", [128, 2, NT, 8]) for n in (0, 1)]
        mparts = sb("mparts", [128, NT, 2, 8], bf16)
        mT = sb("mT", [16, S], bf16)
        P = sb("P", [128, 2, 4, S])
        oT = sb("oT", [128, S])
        rcp = sb("rcp", [128, NT, 4])
        mix = sb("mix", [128, 2, NC, S])
        act2 = sb("act2", [128, NC, S])
        gate_r = sb("gate_r", [128, NT, D])
        c2 = sb("c2", [128, NC, S])

        SC = ctx.enter_context(nc.psum_tensor("SC", [128, 2, S], fp32))
        MX = ctx.enter_context(nc.psum_tensor("MX", [128, 2, S], fp32))
        AV = ctx.enter_context(nc.psum_tensor("AV", [128, S], fp32))
        DN = ctx.enter_context(nc.psum_tensor("DN", [128, DENSE_BANKS, S], fp32))

        sem = {n: ctx.enter_context(nc.semaphore(n)) for n in PER_SEQ}
        for n in ("consts_in", "memsets", "halves", "state_set", "cu_full", "cu_out",
                  "z_in0", "z_in1", "zsum", "ztanh", "zfinal", "z_stored0", "z_stored1"):
            sem[n] = ctx.enter_context(nc.semaphore(n))

        def w(name):
            return W[:, W_NAMES.index(name), :, :]

        def c_(name, c):
            i = COL_NAMES.index(name)
            return col[:, i, c:c + 1]

        credited = ("state", "x3_stored", "z_stored0", "z_stored1")

        class Turn:
            def __init__(self, eng):
                self.eng, self.n, self.i = eng, {}, None

            def done(self, ins, name, by=1):
                self.n[name] = self.n.get(name, 0) + by
                ins.then_inc(sem[name], by)

            def need(self, name, off, n):
                value = self.i * PER_SEQ[name] + (off * PER_SEQ[name] + n + (name in credited))
                if isinstance(value, int):
                    value = min(value, B * PER_SEQ[name] + (name in credited))
                else:
                    assert (LOOP_START + off) * PER_SEQ[name] + n + (name in credited) > 0, name
                if not isinstance(value, int) or value > 0:
                    self.eng.wait_ge(sem[name], value)

            def has(self, off):
                return not isinstance(self.i, int) or 0 <= self.i + off < B

            def steps(self, slot, beat):
                for step in STEPS[slot][beat]:
                    if self.has(step[2]):
                        yield step

            def run(self, body):
                for i in range(-1, LOOP_START):
                    self.i = i
                    body()
                self.n = {}
                with self.eng.Fori(LOOP_START, B - 1) as i:
                    self.i = i
                    body()
                for name, n in self.n.items():
                    assert n == PER_SEQ[name], (name, n, PER_SEQ[name])
                for i in (B - 1, B, B + 1):
                    self.i = i
                    body()

        def bank(step):
            return DN[:, PLACE[step] % DENSE_BANKS, :]

        def token_tiles(ap):
            return ap.rearrange("p (t d) -> p t d", d=D)

        def dram(ap, i):
            if isinstance(i, int):
                return ap[i].rearrange("(t p) d -> p t d", p=128)
            return ap[bass.ds(i, 1)].rearrange("o (t p) d -> p (o t) d", p=128)

        def z_pair(p):
            return mix[:, p].rearrange("p c n -> p (c n)")

        block = ctx.enter_context(nc.Block())

        @block.sync
        def _(sp):
            for dst, src in ((W[:], weights.rearrange("w (c p) n -> p w c n", p=128)),
                             (col[:], columns),
                             (idf[:], ident_f), (idb[:], ident_b), (msk[:], causal),
                             (Qs[0][ROW_EXTRA:ROWS], extra_q[0]), (Qs[1][ROW_EXTRA:ROWS], extra_q[1]),
                             (Ks[0][ROW_EXTRA:ROWS], extra_k), (Ks[1][ROW_EXTRA:ROWS], extra_k)):
                sp.dma_start(dst, src).then_inc(sem["consts_in"], 16)
            for r in range(len(ROW_NAMES)):
                sp.dma_start(row[:, r, :], rows[r:r + 1, :].partition_broadcast(128)).then_inc(sem["consts_in"], 16)
            t = Turn(sp)

            where = {}

            def at(off):
                return where[off]

            def store_parts(layer, off):
                for side in (0, 1):
                    t.need(f"qk_low{layer}", off, 2 * side + 2)
                    t.done(sp.dma_start(parts_dram[layer][side].rearrange("t (c p) n -> p t c n", p=128),
                                        parts[:, side]), "qk"[side] + f"_stored{layer}", 16)

            def load_stack(layer, off, hi):
                if hi:
                    t.need(f"score_full{layer}", off - 1, 32)
                else:
                    t.need(f"q_stored{layer}", off, 16)
                    t.need(f"k_stored{layer}", off, 16)
                heads = slice(8 * hi, 8 * hi + 8)
                for side in (0, 1):
                    src = parts_dram[layer][side]
                    dst = (Qs, Ks)[side][layer]
                    runs = ([(k, p, 1) for k, p in enumerate(K_TERMS)] if side
                            else [(0, 0, 3), (3, 0, 2), (5, 0, 1)])
                    for k, p, m in runs:
                        t.done(sp.dma_start(dst[TERM * k:TERM * (k + m), heads],
                                            src[p:p + m].rearrange("t (d h) n -> (t d) h n", h=H)[:, heads]),
                               ("stack_lo", "stack_hi")[hi] + str(layer), 16)

            def load_max_rows(layer, off, hi):
                t.need(f"maxT_out{layer}", off, hi + 1)
                for part in (0, 1):
                    t.done(sp.dma_start(Qs[layer][ROW_MAX + part:ROW_MAX + part + 1, 8 * hi:8 * hi + 8],
                                        mT[8 * part:8 * part + 8, :]), ("rows_lo", "rows_hi")[hi] + str(layer), 16)

            def slot0():
                if t.has(0):
                    load_max_rows(0, 0, 1)
                if t.has(-1):
                    load_stack(1, -1, 1)
                if t.has(-2):
                    t.need("x3_stored", -3, 16)
                    t.done(sp.dma_start(xres[1][:], dram(x2_dram, at(-2))), "x2_in", 16)
                if t.has(1):
                    t.need("normed1", 0, 4)
                    t.done(sp.dma_start(x_sb[:], dram(x, at(1))), "x_in", 16)
                if t.has(0):
                    t.need("x2_stored", -1, 16)
                    t.need("normed3", -1, 4)
                    t.done(sp.dma_start(xres[0][:], dram(x, at(0))), "res_in", 16)
                if t.has(-1):
                    load_max_rows(1, -1, 0)
                if t.has(-2):
                    t.need("proj_out1", -2, 2)
                    t.done(sp.dma_start(dram(x3_dram, at(-2)), xres[1][:]), "x3_stored", 16)
                    t.need("zo_out1", -2, 2)
                    t.done(sp.dma_start(dram(zo_dram, at(-2)), gate_r[:]), "zo_stored", 16)
                if t.has(1):
                    store_parts(0, 1)
                    load_stack(0, 1, 0)

            def slot1():
                if t.has(-1):
                    load_max_rows(1, -1, 1)
                if t.has(1):
                    load_stack(0, 1, 1)
                    load_max_rows(0, 1, 0)
                if t.has(0):
                    t.need("ffn_out", 0, 2)
                    t.done(sp.dma_start(dram(x2_dram, at(0)), xres[0][:]), "x2_stored", 16)
                    store_parts(1, 0)
                    load_stack(1, 0, 0)

            def turn():
                for off in (-2, 0, 1):
                    where[off] = t.i + off if isinstance(t.i, int) else sp.snap(t.i + off)
                slot0()
                slot1()

            t.run(turn)
            sp.wait_ge(sem["x3_stored"], 16 * B + 1)
            sp.wait_ge(sem["zo_stored"], 16 * B)
            sp.wait_ge(sem["cu_out"], 2)
            with sp.Fori(0, B // 2) as i:
                both = [sp.snap(2 * i), sp.snap(2 * i + 1)]
                for p, n in enumerate(both):
                    sp.wait_ge(sem[f"z_stored{p}"], 16 * i + 1)
                    sp.dma_start(token_tiles(z_pair(p)), dram(zo_dram, n)).then_inc(sem[f"z_in{p}"], 16)
                    sp.dma_start((x_sb, xres[0])[p][:], dram(x3_dram, n)).then_inc(sem[f"z_in{p}"], 16)
                for p, n in enumerate(both):
                    sp.wait_ge(sem["zfinal"], 2 * i + p + 1)
                    sp.dma_start(dram(out, n), (x_sb, xres[0])[p][:])\
                      .then_inc(sem[f"z_stored{p}"], 16)
            for p in (0, 1):
                sp.wait_ge(sem[f"z_stored{p}"], 16 * (B // 2) + 1)

        @block.gpsimd
        def _(pool):
            pool.wait_ge(sem["memsets"], N_MEMSETS)
            pool.wait_ge(sem["consts_in"], CONSTS)
            t = Turn(pool)

            def step(kind, layer, off, k):
                if kind[:4] == "norm":
                    n = kind[4]
                    t.need("moments" + n, off, 4)
                    t.done(pool.tensor_tensor(var_eps[:], mom[:, :, 1], eps[:], ALU.add), "eps" + n)
                    t.need("eps" + n, off, 1)
                    t.done(pool.tensor_tensor(rstd[:], var_eps[:], minus_half[:], ALU.pow), "rstd" + n)
                elif kind == "qk":
                    side, c = k // 2, k % 2
                    t.need(f"qk_out{layer}", off, k + 1)
                    pool.tensor_tensor(wait_cell[:, 0:1], minus_half[:, 0:1], minus_half[:, 0:1], ALU.add)
                    t.done(pool.tensor_copy(parts[:, side, 1, c, :], rest[:, k % 2, :]), f"qk_mid{layer}")
                    t.need(f"qk_mid{layer}", off, k + 1)
                    if k == 3:
                        t.need(f"score_full{layer}", off - 1, 16)
                    t.done(pool.tensor_tensor(parts[:, side, 2, c, :], rest[:, k % 2, :], parts[:, side, 1, c, :],
                                              ALU.subtract), f"qk_low{layer}")
                elif kind == "fk":
                    t.need("fk_out0", off, k + 1)
                    t.done(pool.tensor_tensor(act2[:, k, :], act2[:, k, :], act2[:, k, :], ALU.mult), "square")

            def turn():
                for slot in (0, 1):
                    for beat in range(BEATS):
                        if slot == 0 and beat == 20 and t.has(0):
                            t.need("res_in", 0, 16)
                            for tt in range(NT):
                                ins = pool.tensor_tensor(xres[0][:, tt, :], xres[0][:, tt, :], row[:, 1, :], ALU.add)
                            t.done(ins, "bias_added")
                        for s in t.steps(slot, beat):
                            step(*s)

            t.run(turn)
            pool.wait_ge(sem["cu_out"], 2)
            with pool.Fori(0, B // 2) as i:
                for p in (0, 1):
                    pool.wait_ge(sem[f"z_in{p}"], 32 * i + 32)
                    pool.tensor_tensor(z_pair(p), z_pair(p), h_sb[:].rearrange("p t d -> p (t d)"), ALU.add)\
                        .then_inc(sem["zsum"], 1)

        @block.scalar
        def _(act):
            act.wait_ge(sem["memsets"], N_MEMSETS)
            act.wait_ge(sem["consts_in"], CONSTS)
            act.wait_ge(sem["halves"], N_HALVES)
            t = Turn(act)

            def exp_unit(layer, off, u):
                g, kt, pair = u // 8, u // 2 % 4, u % 2
                if u >= 4 and pair == 0:
                    t.need(f"av_full{layer}", off, u // 2 - 1)
                elif pair == 0:
                    t.need(f"av_full{1 - layer}", off + OTHER_EXP[layer], 15 + u // 2)
                t.need(f"score_full{layer}", off, u + 1)
                n = queries(layer, kt)
                t.done(act.activation(P[:, kt % 2, 2 * pair:2 * pair + 2, 0:n], SC[:, :, 0:n], ACT.Exp, scale=SCALE),
                       f"exp_out{layer}")

            def unload(layer, off, g):
                if g:
                    t.need(f"back_full{layer}", off, g)
                else:
                    t.need(f"back_full{1 - layer}", off + OTHER_EXP[layer], 4)
                t.need(f"av_full{layer}", off, 4 * g + 4)
                t.done(act.activation(oT[:], AV[:], ACT.Copy), f"av_out{layer}")

            def step(kind, layer, off, k):
                o = bank((kind, layer, off, k)) if kind in BANKED else None
                both = slice(2 * k, 2 * k + 2)
                if kind in ("onT", "nT1", "nT2", "nT3", "nT4"):
                    tag = str(layer) if kind == "onT" else ""
                    t.need(kind + "_full" + tag, off, k + 1)
                    t.done(act.activation(hT[:, k, 1:S + 1], o, ACT.Copy), kind + "_out" + tag)
                elif kind == "qk":
                    side, c = k // 2, k % 2
                    t.need(f"qk_full{layer}", off, k + 1)
                    bias = c_(("bq", "bk")[side], c) if layer == 0 else zero_col[:]
                    t.done(act.activation(parts[:, side, 0, c, :], o, ACT.Identity, bias=bias), f"qk_high{layer}")
                elif kind == "fr":
                    if k == 0:
                        t.need("zo_stored", off - 2, 16)
                    t.need("fr_full0", off, k + 1)
                    t.done(act.activation(gate_r[:, both, :], token_tiles(o), ACT.Tanh, scale=0.5), "fr_out0")
                elif kind == "gates":
                    gate, c = k // 2, k % 2
                    t.need("gates_full1", off, k + 1)
                    dst, bias, scale = ((mix[:, 0, c, :], half[:, 0, c:c + 1], 0.5),
                                        (mix[:, 1, c, :], half[:, 1, c:c + 1], 0.5),
                                        (act2[:, c, :], c_("bc", c), 1.0))[gate]
                    t.done(act.activation(dst, o, ACT.Tanh, bias=bias, scale=scale), "gates_out1")
                elif kind == "zo":
                    t.need("zo_full1", off, k + 1)
                    t.done(act.activation(gate_r[:, both, :], token_tiles(o), ACT.Copy), "zo_out1")

            def turn():
                for slot in (0, 1):
                    e_layer, e_off, _, _ = SLOTS[slot]
                    p_layer, p_off, _, _ = SLOTS[1 - slot]
                    before = 0 if slot else -1
                    for beat in range(BEATS):
                        if t.has(e_off):
                            exp_unit(e_layer, e_off, beat)
                        if beat == 1 and t.has(p_off + before):
                            unload(p_layer, p_off + before, 3)
                        if beat in (9, 17, 25) and t.has(e_off):
                            unload(e_layer, e_off, beat // 8 - 1)
                        for s in t.steps(slot, beat):
                            step(*s)

            t.run(turn)
            with act.Fori(0, B // 2) as i:
                for p in (0, 1):
                    act.wait_ge(sem["zsum"], 2 * i + p + 1)
                    act.activation(z_pair(p), z_pair(p), ACT.Tanh).then_inc(sem["ztanh"], 1)

        @block.vector
        def _(dve):
            for buf, value in ((hT[:, :, 0:1], 0.0), (zero_col[:], 0.0), (V[0][:, :, :, HD:32], 1.0),
                               (V[1][:, :, :, HD:32], 1.0), (minus_half[:], -0.5), (c2[:], 0.0), (eps[:], EPS)):
                dve.memset(buf, value).then_inc(sem["memsets"], 1)
            for i, n in enumerate(credited[1:]):
                dve.memset(credit_cell[:, i:i + 1], 0.0).then_inc(sem[n], 1)
            dve.wait_ge(sem["memsets"], N_MEMSETS)
            dve.wait_ge(sem["consts_in"], CONSTS)
            i_mu, i_f = COL_NAMES.index("mu_r"), COL_NAMES.index("bf")
            dve.tensor_scalar(one_minus[:], col[:, i_mu:i_mu + 2, :], -1.0, 1.0, ALU.mult, ALU.add).then_inc(sem["halves"], 1)
            dve.tensor_scalar(half[:], col[:, i_f:i_f + 2, :], 0.5, None, ALU.mult).then_inc(sem["halves"], 1)
            for name in ("uf", "ui", "uc", "uo"):
                dve.tensor_scalar(w(name), w(name), 0.5, None, ALU.mult).then_inc(sem["halves"], 1)
            for c in range(NC):
                dve.tensor_scalar(c2[:, c, :], c2[:, c, :], c_("in_c", c), 2.0, ALU.add, ALU.mult).then_inc(sem["halves"], 1)
            dve.wait_ge(sem["halves"], N_HALVES)
            dve.memset(credit_cell[:, 3:4], 0.0).then_inc(sem["state"], 1)
            t = Turn(dve)

            def norm(n, off, src):
                for tt in range(NT):
                    t.done(dve.bn_stats(stat[:, tt, :], src[:, tt, :]), "stats" + n)
                t.need("stats" + n, off, 4)
                dve.memset(wait_cell[:, 1:2], 0.0)
                for tt in range(NT):
                    t.done(dve.bn_aggr(mom[:, tt, :], stat[:, tt, :]), "moments" + n)

            def normed(n, off, src):
                t.need("rstd" + n, off, 1)
                for tt in range(NT):
                    t.done(dve.tensor_scalar(h_sb[:, tt, :], src[:, tt, :], mom[:, tt, 0:1], rstd[:, tt:tt + 1],
                                             ALU.subtract, ALU.mult), "normed" + n)

            def max_unit(layer, off, u):
                pair, qt = u // 4, u % 4
                t.need(f"max_full{layer}", off, u + 1)
                a = 2 * (pair % 4)
                t.done(dve.reduce_max(mx[layer][:, pair // 4, qt, a:a + 2], MX[:, :, 0:keys(layer, qt)], axis=AX_X),
                       f"max_out{layer}")

            def max_parts(layer, off, hi):
                t.need(f"max_out{layer}", off, 16 * (hi + 1))
                t.done(dve.tensor_scalar(mparts[:, :, 0, :], mx[layer][:, hi], -1.0, None, ALU.mult), f"max_high{layer}")
                t.need(f"max_high{layer}", off, hi + 1)
                t.done(dve.scalar_tensor_tensor(mparts[:, :, 1, :], mx[layer][:, hi], -1.0, mparts[:, :, 0, :],
                                                ALU.mult, ALU.subtract), f"max_low{layer}")

            def step(kind, layer, off, k):
                o = bank((kind, layer, off, k)) if kind in BANKED else None
                both = slice(2 * k, 2 * k + 2)
                if kind == "v":
                    t.need(f"v_full{layer}", off, k + 1)
                    for a in (0, 1):
                        dst = V[layer][:, 2 * k + a, :, 0:HD]
                        src = o[:, a * D:(a + 1) * D].rearrange("p (h d) -> p h d", d=HD)
                        if layer == 0:
                            ins = dve.tensor_tensor(dst, src, row[:, 0, :].rearrange("p (h d) -> p h d", d=HD), ALU.add)
                        else:
                            ins = dve.tensor_copy(dst, src)
                    t.done(ins, f"v_out{layer}")
                elif kind == "qk":
                    side, c = k // 2, k % 2
                    t.need(f"qk_high{layer}", off, k + 1)
                    if k >= 2:
                        t.need(f"qk_low{layer}", off, k - 1)
                    bias = c_(("bq", "bk")[side], c) if layer == 0 else zero_col[:]
                    t.done(dve.scalar_tensor_tensor(rest[:, k % 2, :], o, bias, parts[:, side, 0, c, :],
                                                    ALU.add, ALU.subtract), f"qk_out{layer}")
                elif kind == "maxT":
                    t.need(f"maxT_full{layer}", off, k + 1)
                    t.done(dve.tensor_copy(mT[:], o[0:16, :].bitcast(bf16)[:, 0:S]), f"maxT_out{layer}")
                elif kind == "back":
                    t.need(f"back_full{layer}", off, k + 1)
                    if k:
                        t.need(f"back_out{layer}", off, k)
                    else:
                        t.need(f"back_out{1 - layer}", off + OTHER_EXP[layer], 4)
                    back = o.rearrange("p (t h m) -> p t h m", h=4, m=32)
                    t.done(dve.reciprocal(rcp[:], back[:, :, :, HD]), f"recip{layer}")
                    t.need(f"recip{layer}", off, k + 1)
                    t.done(dve.tensor_tensor(
                        on[layer][:, :, 4 * HD * k:4 * HD * (k + 1)].rearrange("p t (h d) -> p t h d", d=HD),
                        back[:, :, :, 0:HD], rcp[:].unsqueeze(3).to_broadcast([128, NT, 4, HD]), ALU.mult),
                        f"back_out{layer}")
                elif kind == "proj":
                    if k == 0:
                        t.need("x2_in", off, 16) if layer else t.need("bias_added", off, 1)
                    t.need(f"proj_full{layer}", off, k + 1)
                    t.done(dve.tensor_tensor(xres[layer][:, both, :], token_tiles(o), xres[layer][:, both, :], ALU.add),
                           f"proj_out{layer}")
                elif kind == "norm1":
                    t.need("x_in", off, 16)
                    norm("1", off, x_sb)
                elif kind in ("norm2", "norm4"):
                    t.need(f"proj_out{layer}", off, 2)
                    norm(kind[4], off, xres[layer])
                elif kind == "norm3":
                    t.need("ffn_out", off, 2)
                    norm("3", off, xres[0])
                elif kind[:4] == "unit":
                    normed(kind[4], off, x_sb if kind[4] == "1" else xres[layer])
                elif kind == "mix":
                    t.need("nT2_out", off, 2)
                    for n, m in enumerate((1, 0)):
                        for c in range(NC):
                            t.done(dve.tensor_scalar(mix[:, m, c, :], hT[:, c, 1:S + 1],
                                                     c_(("mu_r", "mu_k")[m], c), None, ALU.mult), "shifted_a")
                    for n, m in enumerate((1, 0)):
                        for c in range(NC):
                            t.need("shifted_a", off, 2 * n + c + 1)
                            t.done(dve.scalar_tensor_tensor(mix[:, m, c, :], hT[:, c, 0:S], one_minus[:, m, c:c + 1],
                                                            mix[:, m, c, :], ALU.mult, ALU.add), "shifted")
                elif kind == "fk":
                    t.need("fk_full0", off, k + 1)
                    t.done(dve.tensor_scalar(act2[:, k, :], o, 0.0, None, ALU.max), "fk_out0")
                elif kind == "fv":
                    t.need("fv_full0", off, k + 1)
                    t.need("fr_out0", off, k + 1)
                    t.done(dve.scalar_tensor_tensor(gate_r[:, both, :], gate_r[:, both, :], 1.0, token_tiles(o),
                                                    ALU.add, ALU.mult), "fv_out0")
                    t.need("fv_out0", off, k + 1)
                    t.done(dve.scalar_tensor_tensor(xres[0][:, both, :], gate_r[:, both, :], 0.5, xres[0][:, both, :],
                                                    ALU.mult, ALU.add), "ffn_out")
                elif kind == "recur":
                    t.need("gates_out1", off, 6)
                    t.done(dve.scalar_tensor_tensor(c2[:], mix[:, 0], 1.0, c2[:], ALU.add, ALU.mult), "keep")
                    t.done(dve.scalar_tensor_tensor(act2[:], mix[:, 1], 1.0, act2[:], ALU.add, ALU.mult), "new")
                    t.need("new", off, 1)
                    t.need("keep", off, 1)
                    t.done(dve.scalar_tensor_tensor(c2[:], c2[:], 0.5, act2[:], ALU.mult, ALU.add), "state")

            def turn():
                for slot in (0, 1):
                    e_layer, e_off, m_layer, m_off = SLOTS[slot]
                    p_layer, p_off, pm_layer, pm_off = SLOTS[1 - slot]
                    before = 0 if slot else -1
                    for beat in range(BEATS):
                        if beat == 0 and t.has(pm_off + before):
                            max_parts(pm_layer, pm_off + before, 1)
                        if beat == 18 and t.has(m_off):
                            max_parts(m_layer, m_off, 0)
                        first, second = max_units(slot, beat)
                        if t.has(m_off):
                            for u in first:
                                max_unit(m_layer, m_off, u)
                        if beat:
                            for s in t.steps(slot, beat - 1):
                                step(*s)
                        if t.has(m_off):
                            for u in second:
                                max_unit(m_layer, m_off, u)
                    for s in t.steps(slot, BEATS - 1):
                        step(*s)

            t.run(turn)
            for i in range(2):
                dve.wait_ge(sem["cu_full"], i + 1)
                for a in (0, 1):
                    ins = dve.tensor_tensor(h_sb[:, 2 * i + a, :], DN[:, i, a * D:(a + 1) * D], row[:, 2, :], ALU.add)
                ins.then_inc(sem["cu_out"], 1)
            with dve.Fori(0, B // 2) as i:
                for p in (0, 1):
                    dve.wait_ge(sem["ztanh"], 2 * i + p + 1)
                    dst = (x_sb, xres[0])[p][:].rearrange("p t d -> p (t d)")
                    dve.tensor_tensor(dst, dst, z_pair(p), ALU.add).then_inc(sem["zfinal"], 1)

        @block.tensor
        def _(pe):
            pe.wait_ge(sem["memsets"], N_MEMSETS)
            pe.wait_ge(sem["consts_in"], CONSTS)
            pe.wait_ge(sem["halves"], N_HALVES)
            t = Turn(pe)

            def take_bank(step):
                n = PLACE[step]
                for back in range(DENSE_BANKS, 2 * IN_TURN, DENSE_BANKS):
                    turns, at = divmod(n - back, IN_TURN)
                    old = ORDER[at]
                    if old is not None and t.has(old[2] + turns):
                        name, count = freed_by(old)
                        t.need(name, old[2] + turns, count)
                        break
                return bank(step)

            def transposes(o, src, c):
                for tt in range(NT):
                    ins = pe.transpose(o[:, 128 * tt:128 * tt + 128], src[:, tt, 128 * c:128 * c + 128], idf[:])
                return ins

            def features(o, name, c, rhs, start=True, stop=True):
                for kc in range(NC):
                    ins = pe.matmul(o, w(name)[:, kc, 128 * c:128 * c + 128], rhs(kc),
                                    start=start and kc == 0, stop=stop and kc == NC - 1)
                return ins

            def tokens(o, name, i, lhs):
                for a in (0, 1):
                    for kc in range(NC):
                        ins = pe.matmul(o[:, a * D:(a + 1) * D], lhs(kc, slice(128 * (2 * i + a), 128 * (2 * i + a) + 128)),
                                        w(name)[:, kc, :], start=kc == 0, stop=kc == NC - 1)
                return ins

            def hT_all(kc):
                return hT[:, kc, 1:S + 1]

            def hT_tile(kc, tile):
                return hT[:, kc, 1 + tile.start:1 + tile.stop]

            def step(kind, layer, off, k):
                if kind not in BANKED:
                    return
                L = str(layer)
                o = take_bank((kind, layer, off, k))
                if kind[:2] == "nT":
                    t.need("normed" + kind[2], off, 4)
                    t.done(transposes(o, h_sb, k), kind + "_full")
                elif kind == "onT":
                    t.need("back_out" + L, off, 2 * k + 2)
                    t.done(transposes(o, on[layer], k), "onT_full" + L)
                elif kind == "proj":
                    t.need("onT_out" + L, off, 2)
                    t.done(tokens(o, "o" + L, k, hT_tile), "proj_full" + L)
                elif kind == "qk":
                    t.need(("nT1_out", "nT3_out")[layer], off, 2)
                    t.done(features(o, "qk"[k // 2] + L, k % 2, hT_all), "qk_full" + L)
                elif kind == "v":
                    t.done(tokens(o, "v" + L, k, hT_tile), "v_full" + L)
                elif kind == "fk":
                    t.need("shifted", off, 2)
                    t.done(features(o, "fk", k, lambda kc: mix[:, 1, kc, :]), "fk_full0")
                elif kind == "fr":
                    t.need("shifted", off, 4)
                    t.done(tokens(o, "fr", k, lambda kc, tile: mix[:, 0, kc, tile]), "fr_full0")
                elif kind == "fv":
                    t.need("square", off, 2)
                    t.done(tokens(o, "fv", k, lambda kc, tile: act2[:, kc, tile]), "fv_full0")
                elif kind == "gates":
                    t.need("nT4_out", off, 2)
                    gate, c = "fic"[k // 2], k % 2
                    features(o, "w" + gate, c, hT_all, stop=False)
                    t.need("state", off - 1, 1)
                    t.done(features(o, "u" + gate, c, lambda kc: c2[:, kc, :], start=False), "gates_full1")
                elif kind == "zo":
                    t.done(tokens(o, "wo", k, hT_tile), "zo_full1")
                elif kind == "maxT":
                    t.need("max_low" + L, off, k + 1)
                    for tt in range(NT):
                        ins = pe.transpose(o[0:16, :].bitcast(bf16)[:, 128 * tt:128 * tt + 128],
                                           mparts[:, tt].rearrange("p a h -> p (a h)"), idb[:])
                    t.done(ins, "maxT_full" + L)
                elif kind == "back":
                    t.need("av_out" + L, off, k + 1)
                    for tt in range(NT):
                        ins = pe.transpose(o[:, 128 * tt:128 * tt + 128], oT[:, 128 * tt:128 * tt + 128], idf[:])
                    t.done(ins, "back_full" + L)

            def max_unit(slot, layer, off, u):
                pair, qt = u // 4, u % 4
                if u == 0:
                    t.need(f"stack_lo{layer}", off, 144)
                    t.need(f"max_out{1 - layer}", off + OTHER_MAX[layer], 32)
                else:
                    t.need(f"max_out{layer}", off, u)
                if u == 16:
                    t.need(f"stack_hi{layer}", off, 144)
                n = keys(layer, qt)
                K = ROW_MAX if layer else ROW_EXTRA
                for a in (0, 1):
                    h = 2 * pair + a
                    ins = pe.matmul(MX[:, a, 0:n], Qs[layer][0:K, h, 128 * qt:128 * qt + 128], Ks[layer][0:K, h, 0:n],
                                    start=True, stop=layer == 0)
                    if layer == 1:
                        ins = pe.matmul(MX[:, a, n - 128:n], idb[:], msk[:], start=False, stop=True)
                t.done(ins, f"max_full{layer}")

            def scores(layer, off, u):
                g, kt, pair = u // 8, u // 2 % 4, u % 2
                if u in (0, 16):
                    t.need(f"rows_{'hi' if u else 'lo'}{layer}", off, 32)
                if u:
                    t.need(f"exp_out{layer}", off, u)
                else:
                    t.need(f"exp_out{1 - layer}", off + OTHER_EXP[layer], 32)
                n = queries(layer, kt)
                for a in (0, 1):
                    h = 4 * g + 2 * pair + a
                    ins = pe.matmul(SC[:, a, 0:n], Ks[layer][0:ROWS, h, 128 * kt:128 * kt + 128],
                                    Qs[layer][0:ROWS, h, S - n:S], start=True, stop=layer == 0)
                    if layer == 1:
                        ins = pe.matmul(SC[:, a, 0:128], msk[:], idb[:], start=False, stop=True)
                t.done(ins, f"score_full{layer}")

            def with_values(layer, off, m):
                g, kt = m // 4, m % 4
                t.need(f"exp_out{layer}", off, 2 * m + 2)
                if g and kt == 0:
                    t.need(f"av_out{layer}", off, g)
                elif kt == 0:
                    t.need(f"av_out{1 - layer}", off + OTHER_EXP[layer], 4)
                n = queries(layer, kt)
                for j in range(4):
                    ins = pe.matmul(AV[32 * j:32 * j + 32, S - n:S], V[layer][:, kt, 4 * g + j, :],
                                    P[:, kt % 2, j, 0:n], start=kt == 0, stop=kt == NT - 1)
                t.done(ins, f"av_full{layer}")

            def turn():
                for slot in (0, 1):
                    e_layer, e_off, m_layer, m_off = SLOTS[slot]
                    p_layer, p_off, _, _ = SLOTS[1 - slot]
                    before = 0 if slot else -1
                    for beat in range(BEATS):
                        first, second = max_units(slot, beat)
                        if t.has(m_off):
                            for u in first:
                                max_unit(slot, m_layer, m_off, u)
                        if t.has(e_off):
                            scores(e_layer, e_off, beat)
                        if beat == 0 and t.has(p_off + before):
                            with_values(p_layer, p_off + before, 15)
                        if beat and beat % 2 == 0 and t.has(e_off):
                            with_values(e_layer, e_off, beat // 2 - 1)
                        if t.has(m_off):
                            for u in second:
                                max_unit(slot, m_layer, m_off, u)
                        for s in t.steps(slot, beat):
                            step(*s)

            t.run(turn)
            pe.wait_ge(sem["state"], B + 1)
            pe.wait_ge(sem["zo_out1"], 2 * B)
            for i in range(2):
                tokens(DN[:, i, :], "uo", i, lambda kc, tile: c2[:, kc, tile]).then_inc(sem["cu_full"], 1)


N_MEMSETS = 7
N_HALVES = 8
CONSTS = 16 * 12


def queries(layer, kt):
    return 512 - 128 * kt if layer else 512


def keys(layer, qt):
    return 128 * (qt + 1) if layer else 512


def _split(a, dtype):
    import numpy as np
    parts = []
    for _ in range(3):
        p = a.astype(dtype)
        parts.append(p)
        a = a - p.astype(np.float64)
    return parts


def _constants():
    import numpy as np
    bf = mybir.dt.np(mybir.dt.bfloat16)
    H, S = 16, 512
    ratio = 2.0 ** (-8.0 / H)
    slopes = np.array([ratio ** (i + 1) for i in range(H)], np.float32).astype(np.float64)
    line = 4.0 * slopes[:, None] * np.arange(S)[None, :]
    n = ROWS - ROW_EXTRA
    q = np.zeros((2, n, H, S), bf)
    k = np.zeros((n, H, S), bf)
    for i, (kp, qp) in enumerate(zip(_split(line, bf), _split(-line, bf))):
        q[1, i], k[i] = 1.0, kp
        q[1, 3 + i], k[3 + i] = qp, 1.0
    k[ROWS_ALIBI:] = 1.0
    causal = np.where(np.arange(128)[None, :] > np.arange(128)[:, None], -1e30, 0.0).astype(bf)
    return dict(ident_f=np.eye(128, dtype=np.float32), ident_b=np.eye(128).astype(bf), causal=causal,
                extra_q=q, extra_k=k)


def kernel(**inputs):
    import numpy as np
    import concourse.bacc as bacc
    from concourse.bass_utils import run_bass_kernel_spmd

    a = {n: np.asarray(v) for n, v in inputs.items()}
    d_major = np.arange(256).reshape(16, 16).T.reshape(-1)
    weights = np.stack([
        a["L0_attn_Wq"][:, d_major], a["L0_attn_Wk"][:, d_major], a["L0_attn_Wv"], a["L0_attn_Wo"],
        a["L0_ffn_W_r"].T, a["L0_ffn_W_k"].T, a["L0_ffn_W_v"].T,
        a["L1_attn_q_w"][:, d_major], a["L1_attn_k_w"][:, d_major], a["L1_attn_v_w"], a["L1_attn_o_w"],
        a["L1_ffn_wf"].T, a["L1_ffn_uf"].T, a["L1_ffn_wi"].T, a["L1_ffn_ui"].T,
        a["L1_ffn_wc"].T, a["L1_ffn_uc"].T, a["L1_ffn_wo"].T, a["L1_ffn_uo"].T])
    columns = np.stack([a["L0_attn_bq"][d_major], a["L0_attn_bk"][d_major], a["L0_ffn_mu_r"], a["L0_ffn_mu_k"],
                        a["L1_ffn_bf"], a["L1_ffn_bi"], a["L1_ffn_bc"], a["L1_ffn_in_c"]])
    columns = columns.reshape(len(COL_NAMES), 2, 128).transpose(2, 0, 1)
    rows = np.stack([a["L0_attn_bv"], a["L0_attn_bo"], a["L1_ffn_bo"]])
    arrays = dict(x=a["L0_attn_x"], weights=weights, columns=columns, rows=rows, **_constants())
    arrays = {n: np.ascontiguousarray(v) for n, v in arrays.items()}

    nc = bacc.Bacc("TRN2", target_bir_lowering=False, num_devices=1)
    args = [nc.dram_tensor(n, v.shape, mybir.dt.from_np(v.dtype), kind="ExternalInput").ap()
            for n, v in arrays.items()]
    out = nc.dram_tensor("out", arrays["x"].shape, mybir.dt.float32, kind="ExternalOutput").ap()
    sequence_stack_kernel(nc, *args, out)
    result = run_bass_kernel_spmd(nc, [arrays], core_ids=[0])
    return result.results[0]["out"]
```

```python
import concourse.bass as bass
from concourse import mybir
from contextlib import ExitStack

TERM = 16
Q_TERMS = (0, 1, 2, 0, 1, 0)
K_TERMS = (0, 0, 0, 1, 1, 2)
ROW_EXTRA = 6 * TERM
ROWS_ALIBI = 6
ROW_MAX = ROW_EXTRA + ROWS_ALIBI
ROWS = ROW_MAX + 2

W_NAMES = ("q0", "k0", "v0", "o0", "fr", "fk", "fv", "q1", "k1", "v1", "o1",
           "wf", "uf", "wi", "ui", "wc", "uc", "wo", "uo")
COL_NAMES = ("bq", "bk", "mu_r", "mu_k", "bf", "bi", "bc", "in_c")
ROW_NAMES = ("bv", "bo", "bo_rnn")


FIRST_WEIGHTS = 3
BEATS = 32
HALF_MAX = 20
LOOP_START = 2
B_TOTAL = 16
DENSE_BANKS = 3
LAST_BUFFERS = 8


def _steps():
    table = [[[] for _ in range(BEATS)] for _ in (0, 1)]

    def put(slot, beat, kind, layer, off, index=0):
        table[slot][beat].append((kind, layer, off, index))

    for slot in (0, 1):
        e_layer, e_off, m_layer, m_off = SLOTS[slot]
        p_layer, p_off, pm_layer, pm_off = SLOTS[1 - slot]
        before = 0 if slot else -1
        put(slot, 2, "back", p_layer, p_off + before, 3)
        for g in range(3):
            put(slot, 8 * g + 11, "back", e_layer, e_off, g)
        put(slot, 0, "maxT", pm_layer, pm_off + before, 1)
        put(slot, HALF_MAX, "maxT", m_layer, m_off, 0)
    put(0, 2, "norm1", 0, 1)
    put(0, 3, "unit1", 0, 1)
    for k in (0, 1):
        put(0, k, "v", 1, -1, k)
        put(0, 3 + k, "onT", 1, -2, k)
        put(0, 5 + k, "proj", 1, -2, k)
        put(0, 6 + k, "nT1", 0, 1, k)
        put(0, 10 + k, "nT4", 1, -2, k)
        put(0, 25 + 2 * k, "zo", 1, -2, k)
    put(0, 6, "norm4", 1, -2)
    put(0, 7, "unit4", 1, -2)
    for k, beat in enumerate((8, 9, 17, 18)):
        put(0, beat, "qk", 0, 1, k)
        put(0, beat + 2, "mid", 0, 1, k)
    for k, beat in enumerate((11, 13, 15, 19, 21, 23)):
        put(0, beat, "gates", 1, -2, k)
        put(0, beat + 1, "gates_end", 1, -2, k)
    put(0, 24, "recur", 1, -2, 0)
    put(0, 25, "recur", 1, -2, 1)
    for k in (0, 1):
        put(1, 3 + k, "onT", 0, 0, k)
        put(1, 5 + k, "proj", 0, 0, k)
        put(1, 8 + 4 * k, "v", 0, 1, k)
        put(1, 10 + k, "nT2", 0, 0, k)
        put(1, 14 + k, "fk", 0, 0, k)
        put(1, 16 + k, "fr", 0, 0, k)
        put(1, 18 + k, "fv", 0, 0, k)
        put(1, 23 + k, "nT3", 0, 0, k)
    put(1, 6, "norm2", 0, 0)
    put(1, 7, "unit2", 0, 0)
    put(1, 12, "mix", 0, 0, 0)
    put(1, 13, "mix", 0, 0, 1)
    put(1, 19, "norm3", 0, 0)
    put(1, 20, "unit3", 0, 0)
    for k in range(4):
        put(1, 25 + k, "qk", 1, 0, k)
        put(1, 27 + k, "mid", 1, 0, k)
    return table


SLOTS = ((0, 0, 1, -1), (1, -1, 0, 1))
BANKED = ("v", "onT", "proj", "nT1", "nT2", "nT3", "nT4", "gates", "zo", "qk", "fk", "fr", "fv", "back", "maxT")
STEPS = _steps()
ORDER = [s for slot in STEPS for beat in slot for s in beat if s[0] in BANKED]
PLACE = {s: n for n, s in enumerate(ORDER)}
assert len(PLACE) == len(ORDER)
IN_TURN = -(-len(ORDER) // DENSE_BANKS) * DENSE_BANKS
ORDER += [None] * (IN_TURN - len(ORDER))

OTHER_EXP = (-2, 1)
OTHER_MAX = (-2, 1)

MAX_COUNTS = (
    (0, 0, 0, 0, 0, 0, 1, 0, 1, 1, 1, 2, 1, 2, 1, 2, 1, 2, 1, 2, 1, 2, 1, 2, 1, 2, 0, 1, 1, 1, 1, 1),
    (1, 1, 1, 1, 1, 2, 1, 0, 0, 1, 1, 2, 0, 0, 1, 2, 2, 2, 1, 0, 0, 1, 0, 1, 1, 2, 2, 2, 1, 1, 1, 0))
assert all(len(c) == BEATS and sum(c) == 32 and sum(c[:HALF_MAX]) >= 16 for c in MAX_COUNTS)


def max_units(slot, beat):
    edge = sum(MAX_COUNTS[slot][:beat])
    units = range(edge, edge + MAX_COUNTS[slot][beat])
    return units[:1], units[1:]


PER_SEQ = dict(x_in=16, res_in=16, bias_added=1, x2_stored=16, x2_in=16, x3_stored=16, zo_stored=16,
               shifted_a=4, shifted=4, square=2, ffn_out=2, keep=1, new=1, state=1)
for _n in "1234":
    PER_SEQ.update({"stats" + _n: 4, "moments" + _n: 4, "eps" + _n: 1, "rstd" + _n: 1, "normed" + _n: 4,
                    f"nT{_n}_full": 2, f"nT{_n}_out": 2})
for _l in "01":
    PER_SEQ.update({k + _l: n for k, n in dict(
        v_full=2, v_out=2, onT_full=2, onT_out=2, proj_full=2, proj_out=2, qk_full=4, qk_high=4, qk_out=4,
        qk_mid=4, qk_low=4, back_full=4, recip=4, back_out=4, maxT_full=2, maxT_out=2, max_high=2, max_low=2,
        av_full=16, av_out=4,
        q_stored=16, k_stored=16, stack_lo=144, stack_hi=144, rows_lo=32, rows_hi=32).items()})
for _l in "01":
    for _b in "ab":
        PER_SEQ.update({k + _b + _l: 32 for k in ("max_full", "max_out", "score_full", "exp_out")})
PER_SEQ.update(gates_full1=6, gates_out1=6, zo_full1=2, zo_out1=2, fk_full0=2, fk_out0=2, fr_full0=2, fr_out0=2,
               fv_full0=2, fv_out0=2)


def freed_by(step):
    kind, layer, _, index = step
    name = kind + "_out" if kind[0] == "n" else f"{kind}_out{layer}"
    signals = [(name, index + 1)]
    if kind == "nT2":
        signals.append(("shifted_a", 2 * index + 2))
    return signals


def sequence_stack_kernel(nc, x, weights, columns, rows, ident_f, ident_b, causal, extra_q, extra_k, out):
    fp32, bf16 = mybir.dt.float32, mybir.dt.bfloat16
    ALU, ACT = mybir.AluOpType, mybir.ActivationFunctionType
    AX_X = mybir.AxisListType.X
    B, S, D = x.shape
    assert B == B_TOTAL
    H, HD = 16, 16
    V_HEAD = HD + 1
    V_ROW = V_HEAD * (H - 1) + 32
    NT = S // 128
    NC = D // 128
    EPS = 1e-5
    SCALE = float(HD) ** -0.5

    parts_dram = [[nc.dram_tensor(f"parts_{n}{layer}", (3, NC * 128, S), bf16, kind="Internal").ap() for n in "qk"]
                  for layer in (0, 1)]
    x2_dram = nc.dram_tensor("x_after_layer0", (B, S, D), fp32, kind="Internal").ap()
    x3_dram = nc.dram_tensor("x_after_attention1", (B, S, D), fp32, kind="Internal").ap()
    zo_dram = nc.dram_tensor("output_gate_input", (B, S, D), fp32, kind="Internal").ap()

    ctx = ExitStack()
    with ctx:
        def sb(name, shape, dt=fp32):
            return ctx.enter_context(nc.sbuf_tensor(name, shape, dt))

        W = sb("W", [128, len(W_NAMES), NC, D])
        col = sb("col", [128, len(COL_NAMES), NC])
        half = sb("half", [128, 2, NC])
        one_minus = sb("one_minus", [128, 2, NC])
        row = sb("row", [128, len(ROW_NAMES), D])
        idf = sb("idf", [128, 128])
        idb = sb("idb", [128, 128], bf16)
        msk = sb("msk", [128, 128], bf16)
        zero_col = sb("zero_col", [128, 1])
        x_sb = sb("x_sb", [128, NT, D])
        xres = [sb("xres0", [128, NT, D]), sb("xres1", [128, NT, D])]
        stat = sb("stat", [128, NT, 6])
        mom = sb("mom", [128, NT, 2])
        var_eps = sb("var_eps", [128, NT])
        minus_half = sb("minus_half", [128, NT])
        rstd = sb("rstd", [128, NT])
        eps = sb("eps", [128, NT])
        credit_cell = sb("credit_cell", [128, 2 + LAST_BUFFERS])
        wait_cell = sb("wait_cell", [128, 2])
        h_sb = sb("h_sb", [128, NT, D])
        on = [sb("on0", [128, NT, D]), sb("on1", [128, NT, D])]
        hT = sb("hT", [128, NC, S + 1])
        hN = sb("hN", [128, NC, S])
        rest = sb("rest", [128, 2, S])
        parts = sb("parts", [128, 2, 3, NC, S], bf16)
        Qs = [sb(f"Qs{n}", [128, H, S], bf16) for n in (0, 1)]
        Ks = [sb(f"Ks{n}", [128, H, S], bf16) for n in (0, 1)]
        V = [sb(f"V{n}", [128, NT, V_ROW]) for n in (0, 1)]
        mx = [sb(f"mx{n}", [128, 2, NT, 8]) for n in (0, 1)]
        mparts = sb("mparts", [128, NT, 2, 8], bf16)
        mT = sb("mT", [16, S], bf16)
        P = sb("P", [128, 2, 4, S])
        oT = sb("oT", [128, S])
        rcp = sb("rcp", [128, NT, 4])
        mix = sb("mix", [128, 2, NC, S])
        act2 = sb("act2", [128, NC, S])
        gate_r = sb("gate_r", [128, NT, D])
        c2 = sb("c2", [128, NC, S])

        SC = ctx.enter_context(nc.psum_tensor("SC", [128, 2, S], fp32))
        MX = ctx.enter_context(nc.psum_tensor("MX", [128, 2, S], fp32))
        AV = ctx.enter_context(nc.psum_tensor("AV", [128, S], fp32))
        DN = ctx.enter_context(nc.psum_tensor("DN", [128, DENSE_BANKS, S], fp32))

        sem = {n: ctx.enter_context(nc.semaphore(n)) for n in PER_SEQ}
        for n in ("consts_in", "weights_in", "state_weights", "memsets", "halves", "cu_full", "cu_out",
                  "zsum0", "zsum1", "ztanh", "zfinal",
                  *(f"z_{n}{p}" for n in ("in", "stored") for p in range(LAST_BUFFERS))):
            sem[n] = ctx.enter_context(nc.semaphore(n))

        def w(name):
            return W[:, W_NAMES.index(name), :, :]

        def c_(name, c):
            i = COL_NAMES.index(name)
            return col[:, i, c:c + 1]

        credited = ("state", "x3_stored", *(f"z_stored{p}" for p in range(LAST_BUFFERS)))

        class Turn:
            def __init__(self, eng):
                self.eng, self.n, self.i = eng, {}, None

            def done(self, ins, name, by=1):
                self.n[name] = self.n.get(name, 0) + by
                ins.then_inc(sem[name], by)

            def need(self, name, off, n):
                value = self.i * PER_SEQ[name] + (off * PER_SEQ[name] + n + (name in credited))
                if isinstance(value, int):
                    value = min(value, B * PER_SEQ[name] + (name in credited))
                else:
                    assert (LOOP_START + off) * PER_SEQ[name] + n + (name in credited) > 0, name
                if not isinstance(value, int) or value > 0:
                    self.eng.wait_ge(sem[name], value)

            def has(self, off):
                return not isinstance(self.i, int) or 0 <= self.i + off < B

            def steps(self, slot, beat):
                for step in STEPS[slot][beat]:
                    if self.has(step[2]):
                        yield step

            def run(self, body, behind={}):
                for i in range(-1, LOOP_START):
                    self.i = i
                    body()
                    if i in behind:
                        behind[i]()
                self.n = {}
                with self.eng.Fori(LOOP_START, B - 1) as i:
                    self.i = i
                    body()
                for name, n in self.n.items():
                    assert n == PER_SEQ[name], (name, n, PER_SEQ[name])
                for i in (B - 1, B, B + 1):
                    self.i = i
                    body()

        def bank(step):
            return DN[:, PLACE[step] % DENSE_BANKS, :]

        def heads_of_V(layer, k):
            tiles = V[layer][:, 2 * k:2 * k + 2, 0:V_HEAD * H]
            return tiles.rearrange("p t (h d) -> p t h d", d=V_HEAD)[:, :, :, 0:HD]

        def token_tiles(ap):
            return ap.rearrange("p (t d) -> p t d", d=D)

        def dram(ap, i):
            if isinstance(i, int):
                return ap[i].rearrange("(t p) d -> p t d", p=128)
            return ap[bass.ds(i, 1)].rearrange("o (t p) d -> p (o t) d", p=128)

        def gate_in(p):
            return Ks[p // 4][:].rearrange("p h n -> p (h n)").bitcast(fp32)[:, p % 4 * NT * D:(p % 4 + 1) * NT * D]

        def x_last(p):
            return Qs[p // 4][:].rearrange("p h n -> p (h n)").bitcast(fp32)[:, p % 4 * NT * D:(p % 4 + 1) * NT * D]

        block = ctx.enter_context(nc.Block())

        @block.sync
        def _(sp):
            by_feature = weights.rearrange("w (c p) n -> p w c n", p=128)
            for dst, src in ((W[:, 0:FIRST_WEIGHTS], by_feature[:, 0:FIRST_WEIGHTS]),
                             (col[:], columns),
                             (idf[:], ident_f), (idb[:], ident_b), (msk[:], causal),
                             (Qs[0][ROW_EXTRA:ROWS], extra_q[0]), (Qs[1][ROW_EXTRA:ROWS], extra_q[1]),
                             (Ks[0][ROW_EXTRA:ROWS], extra_k), (Ks[1][ROW_EXTRA:ROWS], extra_k)):
                sp.dma_start(dst, src).then_inc(sem["consts_in"], 16)
            for r in range(len(ROW_NAMES)):
                sp.dma_start(row[:, r, :], rows[r:r + 1, :].partition_broadcast(128)).then_inc(sem["consts_in"], 16)
            sp.dma_start(W[:, FIRST_WEIGHTS:], by_feature[:, FIRST_WEIGHTS:]).then_inc(sem["weights_in"], 16)
            t = Turn(sp)

            where = {}

            def at(off):
                return where[off]

            def store_parts(layer, off, sides=(0, 1)):
                for side in sides:
                    t.need(f"qk_low{layer}", off, 2 * side + 2)
                    t.done(sp.dma_start(parts_dram[layer][side].rearrange("t (c p) n -> p t c n", p=128),
                                        parts[:, side]), "qk"[side] + f"_stored{layer}", 16)

            def load_stack(layer, off, hi):
                if hi:
                    for b in "ab":
                        t.need(f"score_full{b}{layer}", off - 1, 32)
                else:
                    t.need(f"q_stored{layer}", off, 16)
                    t.need(f"k_stored{layer}", off, 16)
                heads = slice(8 * hi, 8 * hi + 8)
                for side in (0, 1):
                    src = parts_dram[layer][side]
                    dst = (Qs, Ks)[side][layer]
                    runs = ([(k, p, 1) for k, p in enumerate(K_TERMS)] if side
                            else [(0, 0, 3), (3, 0, 2), (5, 0, 1)])
                    for k, p, m in runs:
                        t.done(sp.dma_start(dst[TERM * k:TERM * (k + m), heads],
                                            src[p:p + m].rearrange("t (d h) n -> (t d) h n", h=H)[:, heads]),
                               ("stack_lo", "stack_hi")[hi] + str(layer), 16)

            def load_max_rows(layer, off, hi):
                t.need(f"maxT_out{layer}", off, hi + 1)
                for part in (0, 1):
                    t.done(sp.dma_start(Qs[layer][ROW_MAX + part:ROW_MAX + part + 1, 8 * hi:8 * hi + 8],
                                        mT[8 * part:8 * part + 8, :]), ("rows_lo", "rows_hi")[hi] + str(layer), 16)

            def load_last(n):
                p = n % LAST_BUFFERS
                sp.dma_start(token_tiles(gate_in(p)), dram(zo_dram, n)).then_inc(sem[f"z_in{p}"], 16)
                sp.dma_start(token_tiles(x_last(p)), dram(x3_dram, n)).then_inc(sem[f"z_in{p}"], 16)

            def first_of_last_pass():
                for b in "ab":
                    for layer in (0, 1):
                        sp.wait_ge(sem[f"score_full{b}{layer}"], 32 * B)
                        sp.wait_ge(sem[f"max_full{b}{layer}"], 32 * B)
                sp.wait_ge(sem["x3_stored"], 16 * LAST_BUFFERS + 1)
                sp.wait_ge(sem["zo_stored"], 16 * LAST_BUFFERS)
                for n in range(LAST_BUFFERS):
                    load_last(n)

            def slot0():
                if t.has(0):
                    load_max_rows(0, 0, 1)
                if t.has(-1):
                    load_stack(1, -1, 1)
                if t.has(0):
                    t.need("x2_stored", -1, 16)
                    t.done(sp.dma_start(xres[0][:], dram(x, at(0))), "res_in", 16)
                if t.has(1):
                    store_parts(0, 1, (0,))
                if t.has(-1):
                    load_max_rows(1, -1, 0)
                if t.has(-2):
                    t.need("proj_out1", -2, 2)
                    t.done(sp.dma_start(dram(x3_dram, at(-2)), xres[1][:]), "x3_stored", 16)
                if t.has(1):
                    store_parts(0, 1, (1,))
                    load_stack(0, 1, 0)
                if t.has(-2):
                    t.need("zo_out1", -2, 2)
                    t.done(sp.dma_start(dram(zo_dram, at(-2)), gate_r[:]), "zo_stored", 16)

            def slot1():
                if t.has(-1):
                    load_max_rows(1, -1, 1)
                if t.has(1):
                    load_stack(0, 1, 1)
                    load_max_rows(0, 1, 0)
                if t.has(-1):
                    t.need("x3_stored", -2, 16)
                    t.done(sp.dma_start(xres[1][:], dram(x2_dram, at(-1))), "x2_in", 16)
                if t.has(0):
                    t.need("normed3", 0, 4)
                    t.done(sp.dma_start(dram(x2_dram, at(0)), xres[0][:]), "x2_stored", 16)
                    store_parts(1, 0)
                    load_stack(1, 0, 0)

            def turn():
                for off in (-2, -1, 0):
                    where[off] = t.i + off if isinstance(t.i, int) else sp.snap(t.i + off)
                if isinstance(t.i, int) and t.i == B + 1:
                    first_of_last_pass()
                slot0()
                slot1()

            t.run(turn)
            sp.wait_ge(sem["x3_stored"], 16 * B + 1)
            sp.wait_ge(sem["zo_stored"], 16 * B)
            for n in range(LAST_BUFFERS, B):
                sp.wait_ge(sem[f"z_stored{n % LAST_BUFFERS}"], 16 * (n // LAST_BUFFERS) + 1)
                load_last(n)
            for p in range(LAST_BUFFERS):
                sp.wait_ge(sem[f"z_stored{p}"], 16 * (B // LAST_BUFFERS) + 1)

        @block.gpsimd
        def _(pool):
            pool.wait_ge(sem["memsets"], N_MEMSETS)
            pool.wait_ge(sem["consts_in"], CONSTS)
            t = Turn(pool)

            def step(kind, layer, off, k):
                if kind[:4] == "norm":
                    n = kind[4]
                    t.need("moments" + n, off, 4)
                    t.done(pool.tensor_tensor(var_eps[:], mom[:, :, 1], eps[:], ALU.add), "eps" + n)
                    t.need("eps" + n, off, 1)
                    t.done(pool.tensor_tensor(rstd[:], var_eps[:], minus_half[:], ALU.pow), "rstd" + n)
                elif kind == "mid":
                    side, c = k // 2, k % 2
                    t.need(f"qk_mid{layer}", off, k + 1)
                    if k == 3:
                        for b in "ab":
                            t.need(f"score_full{b}{layer}", off - 1, 16)
                    t.done(pool.tensor_tensor(parts[:, side, 2, c, :], rest[:, k % 2, :], parts[:, side, 1, c, :],
                                              ALU.subtract), f"qk_low{layer}")
                elif kind == "fk":
                    t.need("fk_out0", off, k + 1)
                    t.done(pool.tensor_tensor(act2[:, k, :], act2[:, k, :], act2[:, k, :], ALU.mult), "square")

            def turn():
                for slot in (0, 1):
                    for beat in range(BEATS):
                        if slot == 0 and beat == 20 and t.has(0):
                            t.need("res_in", 0, 16)
                            for tt in range(NT):
                                ins = pool.tensor_tensor(xres[0][:, tt, :], xres[0][:, tt, :], row[:, 1, :], ALU.add)
                            t.done(ins, "bias_added")
                        for s in t.steps(slot, beat):
                            step(*s)

            t.run(turn)
            pool.wait_ge(sem["cu_out"], 2)
            with pool.Fori(0, B // LAST_BUFFERS) as i:
                for p in range(0, LAST_BUFFERS, 2):
                    pool.wait_ge(sem[f"z_in{p}"], 32 * i + 32)
                    pool.tensor_tensor(gate_in(p), gate_in(p), h_sb[:].rearrange("p t d -> p (t d)"), ALU.add)\
                        .then_inc(sem["zsum0"], 1)

        @block.scalar
        def _(act):
            act.dma_start(x_sb[:], dram(x, 0)).then_inc(sem["x_in"], 16)
            act.wait_ge(sem["memsets"], N_MEMSETS)
            act.wait_ge(sem["consts_in"], CONSTS)
            act.wait_ge(sem["halves"], N_HALVES)
            t = Turn(act)

            def exp_unit(layer, off, u):
                g, kt, pair = u // 8, u // 2 % 4, u % 2
                if u >= 4 and pair == 0:
                    t.need(f"av_full{layer}", off, u // 2 - 1)
                elif pair == 0:
                    t.need(f"av_full{1 - layer}", off + OTHER_EXP[layer], 15 + u // 2)
                n = queries(layer, kt)
                for a in (0, 1):
                    t.need(f"score_full{'ab'[a]}{layer}", off, u + 1)
                    t.done(act.activation(P[:, kt % 2, 2 * pair + a, 0:n], SC[:, a, 0:n], ACT.Exp, scale=SCALE),
                           f"exp_out{'ab'[a]}{layer}")

            def unload(layer, off, g):
                if g:
                    t.need(f"back_full{layer}", off, g)
                else:
                    t.need(f"back_full{1 - layer}", off + OTHER_EXP[layer], 4)
                t.need(f"av_full{layer}", off, 4 * g + 4)
                t.done(act.activation(oT[:], AV[:], ACT.Copy), f"av_out{layer}")

            def step(kind, layer, off, k):
                o = bank((kind, layer, off, k)) if kind in BANKED else None
                both = slice(2 * k, 2 * k + 2)
                if kind in ("onT", "nT1", "nT2", "nT3", "nT4"):
                    tag = str(layer) if kind == "onT" else ""
                    t.need(kind + "_full" + tag, off, k + 1)
                    dst = hN[:, k, :] if kind in ("nT1", "nT3") else hT[:, k, 1:S + 1]
                    t.done(act.activation(dst, o, ACT.Copy), kind + "_out" + tag)
                    if kind == "nT2":
                        for m in (1, 0):
                            t.done(act.activation(mix[:, m, k, :], o, ACT.Copy, scale=c_(("mu_r", "mu_k")[m], k)),
                                   "shifted_a")
                elif kind == "qk":
                    side, c = k // 2, k % 2
                    t.need(f"qk_full{layer}", off, k + 1)
                    bias = c_(("bq", "bk")[side], c) if layer == 0 else zero_col[:]
                    t.done(act.activation(parts[:, side, 0, c, :], o, ACT.Identity, bias=bias), f"qk_high{layer}")
                elif kind == "maxT":
                    t.need(f"maxT_full{layer}", off, k + 1)
                    t.done(act.activation(mT[:], o[0:16, :].bitcast(bf16)[:, 0:S], ACT.Copy), f"maxT_out{layer}")
                elif kind == "v" and layer == 1:
                    t.need("v_full1", off, k + 1)
                    t.done(act.activation(heads_of_V(1, k), o.rearrange("p (t h d) -> p t h d", t=2, d=HD), ACT.Copy),
                           "v_out1")
                elif kind == "mid":
                    t.need(f"qk_out{layer}", off, k + 1)
                    t.done(act.activation(parts[:, k // 2, 1, k % 2, :], rest[:, k % 2, :], ACT.Copy), f"qk_mid{layer}")
                elif kind == "fr":
                    if k == 0:
                        t.need("zo_stored", off - 2, 16)
                    t.need("fr_full0", off, k + 1)
                    t.done(act.activation(gate_r[:, both, :], token_tiles(o), ACT.Tanh, scale=0.5), "fr_out0")
                elif kind == "gates_end":
                    gate, c = k // 2, k % 2
                    o = bank(("gates", layer, off, k))
                    t.need("gates_full1", off, k + 1)
                    dst, bias, scale = ((mix[:, 0, c, :], half[:, 0, c:c + 1], 0.5),
                                        (mix[:, 1, c, :], half[:, 1, c:c + 1], 0.5),
                                        (act2[:, c, :], c_("bc", c), 1.0))[gate]
                    t.done(act.activation(dst, o, ACT.Tanh, bias=bias, scale=scale), "gates_out1")
                elif kind == "zo":
                    t.need("zo_full1", off, k + 1)
                    t.done(act.activation(gate_r[:, both, :], token_tiles(o), ACT.Copy), "zo_out1")

            def turn():
                for slot in (0, 1):
                    e_layer, e_off, _, _ = SLOTS[slot]
                    p_layer, p_off, _, _ = SLOTS[1 - slot]
                    before = 0 if slot else -1
                    if slot == 0 and t.has(0) and t.has(1):
                        t.need("normed1", 0, 4)
                        t.done(act.dma_start(x_sb[:], dram(x, t.i + 1 if isinstance(t.i, int) else act.snap(t.i + 1))),
                               "x_in", 16)
                    for beat in range(BEATS):
                        if t.has(e_off):
                            exp_unit(e_layer, e_off, beat)
                        if beat == 1 and t.has(p_off + before):
                            unload(p_layer, p_off + before, 3)
                        if beat in (9, 17, 25) and t.has(e_off):
                            unload(e_layer, e_off, beat // 8 - 1)
                        for s in t.steps(slot, beat):
                            step(*s)

            t.run(turn)
            with act.Fori(0, B // LAST_BUFFERS) as i:
                numbers = [act.snap(LAST_BUFFERS * i + p) for p in range(LAST_BUFFERS)]

                def store(p):
                    act.wait_ge(sem["zfinal"], LAST_BUFFERS * i + p + 1)
                    act.dma_start(dram(out, numbers[p]), token_tiles(x_last(p))).then_inc(sem[f"z_stored{p}"], 16)

                for p in range(LAST_BUFFERS):
                    act.wait_ge(sem[f"zsum{p % 2}"], LAST_BUFFERS // 2 * i + p // 2 + 1)
                    act.activation(gate_in(p), gate_in(p), ACT.Tanh).then_inc(sem["ztanh"], 1)
                    if p:
                        store(p - 1)
                store(LAST_BUFFERS - 1)

        @block.vector
        def _(dve):
            for buf, value in ((hT[:, :, 0:1], 0.0), (zero_col[:], 0.0), (V[0][:], 1.0), (V[1][:], 1.0), (minus_half[:], -0.5), (c2[:], 0.0), (eps[:], EPS)):
                dve.memset(buf, value).then_inc(sem["memsets"], 1)
            for i, n in enumerate(credited[1:]):
                dve.memset(credit_cell[:, i:i + 1], 0.0).then_inc(sem[n], 1)
            dve.wait_ge(sem["memsets"], N_MEMSETS)
            dve.wait_ge(sem["consts_in"], CONSTS)
            i_mu, i_f = COL_NAMES.index("mu_r"), COL_NAMES.index("bf")
            dve.tensor_scalar(one_minus[:], col[:, i_mu:i_mu + 2, :], -1.0, 1.0, ALU.mult, ALU.add).then_inc(sem["halves"], 1)
            dve.tensor_scalar(half[:], col[:, i_f:i_f + 2, :], 0.5, None, ALU.mult).then_inc(sem["halves"], 1)
            for c in range(NC):
                dve.tensor_scalar(c2[:, c, :], c2[:, c, :], c_("in_c", c), 2.0, ALU.add, ALU.mult).then_inc(sem["halves"], 1)
            dve.wait_ge(sem["halves"], N_HALVES)
            dve.memset(credit_cell[:, 1 + LAST_BUFFERS:2 + LAST_BUFFERS], 0.0).then_inc(sem["state"], 1)

            def halve_state_weights():
                dve.wait_ge(sem["weights_in"], 16)
                for name in ("uf", "ui", "uc", "uo"):
                    dve.tensor_scalar(w(name), w(name), 0.5, None, ALU.mult).then_inc(sem["state_weights"], 1)

            t = Turn(dve)

            def stats(n, off, src, tiles):
                for tt in tiles:
                    t.done(dve.bn_stats(stat[:, tt, :], src[:, tt, :]), "stats" + n)

            def moments(n, off):
                t.need("stats" + n, off, 4)
                dve.memset(wait_cell[:, 1:2], 0.0)
                for tt in range(NT):
                    t.done(dve.bn_aggr(mom[:, tt, :], stat[:, tt, :]), "moments" + n)

            def normed(n, off, src):
                t.need("rstd" + n, off, 1)
                for tt in range(NT):
                    t.done(dve.tensor_scalar(h_sb[:, tt, :], src[:, tt, :], mom[:, tt, 0:1], rstd[:, tt:tt + 1],
                                             ALU.subtract, ALU.mult), "normed" + n)

            def max_unit(layer, off, u):
                pair, qt = u // 4, u % 4
                for a in (0, 1):
                    t.need(f"max_full{'ab'[a]}{layer}", off, u + 1)
                    h = 2 * (pair % 4) + a
                    t.done(dve.reduce_max(mx[layer][:, pair // 4, qt, h:h + 1], MX[:, a, 0:keys(layer, qt)], axis=AX_X),
                           f"max_out{'ab'[a]}{layer}")

            def max_parts(layer, off, hi):
                for b in "ab":
                    t.need(f"max_out{b}{layer}", off, 16 * (hi + 1))
                t.done(dve.tensor_scalar(mparts[:, :, 0, :], mx[layer][:, hi], -1.0, None, ALU.mult), f"max_high{layer}")
                t.need(f"max_high{layer}", off, hi + 1)
                t.done(dve.scalar_tensor_tensor(mparts[:, :, 1, :], mx[layer][:, hi], -1.0, mparts[:, :, 0, :],
                                                ALU.mult, ALU.subtract), f"max_low{layer}")

            def step(kind, layer, off, k):
                o = bank((kind, layer, off, k)) if kind in BANKED else None
                both = slice(2 * k, 2 * k + 2)
                if kind == "v" and layer == 0:
                    t.need("v_full0", off, k + 1)
                    for a in (0, 1):
                        ins = dve.tensor_tensor(heads_of_V(0, k)[:, a],
                                                o[:, a * D:(a + 1) * D].rearrange("p (h d) -> p h d", d=HD),
                                                row[:, 0, :].rearrange("p (h d) -> p h d", d=HD), ALU.add)
                    t.done(ins, "v_out0")
                elif kind == "qk":
                    side, c = k // 2, k % 2
                    t.need(f"qk_high{layer}", off, k + 1)
                    if k >= 2:
                        t.need(f"qk_low{layer}", off, k - 1)
                    bias = c_(("bq", "bk")[side], c) if layer == 0 else zero_col[:]
                    t.done(dve.scalar_tensor_tensor(rest[:, k % 2, :], o, bias, parts[:, side, 0, c, :],
                                                    ALU.add, ALU.subtract), f"qk_out{layer}")
                elif kind == "back":
                    t.need(f"back_full{layer}", off, k + 1)
                    if k:
                        t.need(f"back_out{layer}", off, k)
                    else:
                        t.need(f"back_out{1 - layer}", off + OTHER_EXP[layer], 4)
                    back = o.rearrange("p (t h m) -> p t h m", h=4, m=32)
                    t.done(dve.reciprocal(rcp[:], back[:, :, :, HD]), f"recip{layer}")
                    t.need(f"recip{layer}", off, k + 1)
                    t.done(dve.tensor_tensor(
                        on[layer][:, :, 4 * HD * k:4 * HD * (k + 1)].rearrange("p t (h d) -> p t h d", d=HD),
                        back[:, :, :, 0:HD], rcp[:].unsqueeze(3).to_broadcast([128, NT, 4, HD]), ALU.mult),
                        f"back_out{layer}")
                elif kind == "proj":
                    if k == 0:
                        t.need("x2_in", off, 16) if layer else t.need("bias_added", off, 1)
                    t.need(f"proj_full{layer}", off, k + 1)
                    t.done(dve.tensor_tensor(xres[layer][:, both, :], token_tiles(o), xres[layer][:, both, :], ALU.add),
                           f"proj_out{layer}")
                    t.need(f"proj_out{layer}", off, k + 1)
                    stats("24"[layer], off, xres[layer], (2 * k, 2 * k + 1))
                elif kind[:4] == "norm":
                    if kind == "norm1":
                        t.need("x_in", off, 16)
                        stats("1", off, x_sb, range(NT))
                    moments(kind[4], off)
                elif kind[:4] == "unit":
                    normed(kind[4], off, x_sb if kind[4] == "1" else xres[layer])
                elif kind == "mix":
                    t.need("nT2_out", off, 2)
                    t.need("shifted_a", off, 3 + k)
                    m = 1 - k
                    for c in range(NC):
                        t.done(dve.scalar_tensor_tensor(mix[:, m, c, :], hT[:, c, 0:S], one_minus[:, m, c:c + 1],
                                                        mix[:, m, c, :], ALU.mult, ALU.add), "shifted")
                elif kind == "fk":
                    t.need("fk_full0", off, k + 1)
                    t.done(dve.tensor_scalar(act2[:, k, :], o, 0.0, None, ALU.max), "fk_out0")
                elif kind == "fv":
                    t.need("fv_full0", off, k + 1)
                    t.need("fr_out0", off, k + 1)
                    t.done(dve.scalar_tensor_tensor(gate_r[:, both, :], gate_r[:, both, :], 1.0, token_tiles(o),
                                                    ALU.add, ALU.mult), "fv_out0")
                    t.need("fv_out0", off, k + 1)
                    t.done(dve.scalar_tensor_tensor(xres[0][:, both, :], gate_r[:, both, :], 0.5, xres[0][:, both, :],
                                                    ALU.mult, ALU.add), "ffn_out")
                    t.need("ffn_out", off, k + 1)
                    stats("3", off, xres[0], (2 * k, 2 * k + 1))
                elif kind == "recur":
                    if k == 1:
                        t.need("new", off, 1)
                        t.need("keep", off, 1)
                        t.done(dve.scalar_tensor_tensor(c2[:], c2[:], 0.5, act2[:], ALU.mult, ALU.add), "state")
                        return
                    t.need("gates_out1", off, 6)
                    t.done(dve.scalar_tensor_tensor(c2[:], mix[:, 0], 1.0, c2[:], ALU.add, ALU.mult), "keep")
                    t.done(dve.scalar_tensor_tensor(act2[:], mix[:, 1], 1.0, act2[:], ALU.add, ALU.mult), "new")

            def turn():
                for slot in (0, 1):
                    e_layer, e_off, m_layer, m_off = SLOTS[slot]
                    p_layer, p_off, pm_layer, pm_off = SLOTS[1 - slot]
                    before = 0 if slot else -1
                    for beat in range(BEATS):
                        if beat == 0 and t.has(pm_off + before):
                            max_parts(pm_layer, pm_off + before, 1)
                        if beat == HALF_MAX and t.has(m_off):
                            max_parts(m_layer, m_off, 0)
                        first, second = max_units(slot, beat)
                        if t.has(m_off):
                            for u in first:
                                max_unit(m_layer, m_off, u)
                        if beat:
                            for s in t.steps(slot, beat - 1):
                                step(*s)
                        if t.has(m_off):
                            for u in second:
                                max_unit(m_layer, m_off, u)
                    for s in t.steps(slot, BEATS - 1):
                        step(*s)

            t.run(turn, {-1: halve_state_weights})
            for i in range(2):
                dve.wait_ge(sem["cu_full"], i + 1)
                for a in (0, 1):
                    ins = dve.tensor_tensor(h_sb[:, 2 * i + a, :], DN[:, i, a * D:(a + 1) * D], row[:, 2, :], ALU.add)
                ins.then_inc(sem["cu_out"], 1)
            dve.wait_ge(sem["cu_out"], 2)
            with dve.Fori(0, B // LAST_BUFFERS) as i:
                def last_sum(p):
                    dve.wait_ge(sem["ztanh"], LAST_BUFFERS * i + p + 1)
                    dve.tensor_tensor(x_last(p), x_last(p), gate_in(p), ALU.add).then_inc(sem["zfinal"], 1)

                for p in range(LAST_BUFFERS):
                    if p % 2:
                        dve.wait_ge(sem[f"z_in{p}"], 32 * i + 32)
                        dve.tensor_tensor(gate_in(p), gate_in(p), h_sb[:].rearrange("p t d -> p (t d)"), ALU.add)\
                            .then_inc(sem["zsum1"], 1)
                    if p:
                        last_sum(p - 1)
                last_sum(LAST_BUFFERS - 1)

        @block.tensor
        def _(pe):
            pe.wait_ge(sem["memsets"], N_MEMSETS)
            pe.wait_ge(sem["consts_in"], CONSTS)
            pe.wait_ge(sem["halves"], N_HALVES)
            t = Turn(pe)

            def take_bank(step):
                n = PLACE[step]
                for back in range(DENSE_BANKS, 2 * IN_TURN, DENSE_BANKS):
                    turns, at = divmod(n - back, IN_TURN)
                    old = ORDER[at]
                    if old is not None and t.has(old[2] + turns):
                        for name, count in freed_by(old):
                            t.need(name, old[2] + turns, count)
                        break
                return bank(step)

            def transposes(o, src, c):
                for tt in range(NT):
                    ins = pe.transpose(o[:, 128 * tt:128 * tt + 128], src[:, tt, 128 * c:128 * c + 128], idf[:])
                return ins

            def features(o, name, c, rhs, start=True, stop=True):
                for kc in range(NC):
                    ins = pe.matmul(o, w(name)[:, kc, 128 * c:128 * c + 128], rhs(kc),
                                    start=start and kc == 0, stop=stop and kc == NC - 1)
                return ins

            def tokens(o, name, i, lhs):
                for a in (0, 1):
                    for kc in range(NC):
                        ins = pe.matmul(o[:, a * D:(a + 1) * D], lhs(kc, slice(128 * (2 * i + a), 128 * (2 * i + a) + 128)),
                                        w(name)[:, kc, :], start=kc == 0, stop=kc == NC - 1)
                return ins

            def hT_all(kc):
                return hT[:, kc, 1:S + 1]

            def hN_all(kc):
                return hN[:, kc, :]

            def hN_tile(kc, tile):
                return hN[:, kc, tile]

            def hT_tile(kc, tile):
                return hT[:, kc, 1 + tile.start:1 + tile.stop]

            def step(kind, layer, off, k):
                L = str(layer)
                if kind == "gates_end":
                    t.need("nT4_out", off, 2)
                    t.done(features(bank(("gates", layer, off, k)), "w" + "fic"[k // 2], k % 2, hT_all, start=False),
                           "gates_full1")
                if kind not in BANKED:
                    return
                o = take_bank((kind, layer, off, k))
                if kind[:2] == "nT":
                    t.need("normed" + kind[2], off, 4)
                    t.done(transposes(o, h_sb, k), kind + "_full")
                elif kind == "onT":
                    t.need("back_out" + L, off, 2 * k + 2)
                    t.done(transposes(o, on[layer], k), "onT_full" + L)
                elif kind == "proj":
                    t.need("onT_out" + L, off, 2)
                    t.done(tokens(o, "o" + L, k, hT_tile), "proj_full" + L)
                elif kind == "qk":
                    t.need(("nT1_out", "nT3_out")[layer], off, 2)
                    t.done(features(o, "qk"[k // 2] + L, k % 2, hN_all), "qk_full" + L)
                elif kind == "v":
                    t.done(tokens(o, "v" + L, k, hN_tile), "v_full" + L)
                elif kind == "fk":
                    t.need("shifted", off, 2)
                    t.done(features(o, "fk", k, lambda kc: mix[:, 1, kc, :]), "fk_full0")
                elif kind == "fr":
                    t.need("shifted", off, 4)
                    t.done(tokens(o, "fr", k, lambda kc, tile: mix[:, 0, kc, tile]), "fr_full0")
                elif kind == "fv":
                    t.need("square", off, 2)
                    t.done(tokens(o, "fv", k, lambda kc, tile: act2[:, kc, tile]), "fv_full0")
                elif kind == "gates":
                    t.need("state", off - 1, 1)
                    features(o, "u" + "fic"[k // 2], k % 2, lambda kc: c2[:, kc, :], stop=False)
                elif kind == "zo":
                    t.done(tokens(o, "wo", k, hT_tile), "zo_full1")
                elif kind == "maxT":
                    t.need("max_low" + L, off, k + 1)
                    for tt in range(NT):
                        ins = pe.transpose(o[0:16, :].bitcast(bf16)[:, 128 * tt:128 * tt + 128],
                                           mparts[:, tt].rearrange("p a h -> p (a h)"), idb[:])
                    t.done(ins, "maxT_full" + L)
                elif kind == "back":
                    t.need("av_out" + L, off, k + 1)
                    for tt in range(NT):
                        ins = pe.transpose(o[:, 128 * tt:128 * tt + 128], oT[:, 128 * tt:128 * tt + 128], idf[:])
                    t.done(ins, "back_full" + L)

            def max_scores(layer, off, u, a):
                pair, qt = u // 4, u % 4
                if u == a == 0:
                    t.need(f"stack_lo{layer}", off, 144)
                if u == 16 and a == 0:
                    t.need(f"stack_hi{layer}", off, 144)
                if u:
                    t.need(f"max_out{'ab'[a]}{layer}", off, u)
                else:
                    t.need(f"max_out{'ab'[a]}{1 - layer}", off + OTHER_MAX[layer], 32)
                n = keys(layer, qt)
                K = ROW_MAX if layer else ROW_EXTRA
                h = 2 * pair + a
                ins = pe.matmul(MX[:, a, 0:n], Qs[layer][0:K, h, 128 * qt:128 * qt + 128], Ks[layer][0:K, h, 0:n],
                                start=True, stop=layer == 0)
                if layer == 1:
                    ins = pe.matmul(MX[:, a, n - 128:n], idb[:], msk[:], start=False, stop=True)
                t.done(ins, f"max_full{'ab'[a]}{layer}")

            def exp_scores(layer, off, u, a):
                g, kt, pair = u // 8, u // 2 % 4, u % 2
                if u in (0, 16) and a == 0:
                    t.need(f"rows_{'hi' if u else 'lo'}{layer}", off, 32)
                if u:
                    t.need(f"exp_out{'ab'[a]}{layer}", off, u)
                else:
                    t.need(f"exp_out{'ab'[a]}{1 - layer}", off + OTHER_EXP[layer], 32)
                n = queries(layer, kt)
                h = 4 * g + 2 * pair + a
                ins = pe.matmul(SC[:, a, 0:n], Ks[layer][0:ROWS, h, 128 * kt:128 * kt + 128],
                                Qs[layer][0:ROWS, h, S - n:S], start=True, stop=layer == 0)
                if layer == 1:
                    ins = pe.matmul(SC[:, a, 0:128], msk[:], idb[:], start=False, stop=True)
                t.done(ins, f"score_full{'ab'[a]}{layer}")

            def with_values(layer, off, m):
                g, kt = m // 4, m % 4
                for b in "ab":
                    t.need(f"exp_out{b}{layer}", off, 2 * m + 2)
                if g and kt == 0:
                    t.need(f"av_out{layer}", off, g)
                elif kt == 0:
                    t.need(f"av_out{1 - layer}", off + OTHER_EXP[layer], 4)
                n = queries(layer, kt)
                for j in range(4):
                    ins = pe.matmul(AV[32 * j:32 * j + 32, S - n:S], V[layer][:, kt, V_HEAD * (4 * g + j):V_HEAD * (4 * g + j) + 32],
                                    P[:, kt % 2, j, 0:n], start=kt == 0, stop=kt == NT - 1)
                t.done(ins, f"av_full{layer}")

            def turn():
                for slot in (0, 1):
                    e_layer, e_off, m_layer, m_off = SLOTS[slot]
                    p_layer, p_off, _, _ = SLOTS[1 - slot]
                    before = 0 if slot else -1
                    for beat in range(BEATS):
                        first, second = max_units(slot, beat)
                        for a in (0, 1):
                            if t.has(e_off):
                                exp_scores(e_layer, e_off, beat, a)
                        if beat == 0 and t.has(p_off + before):
                            with_values(p_layer, p_off + before, 15)
                        if beat and beat % 2 == 0 and t.has(e_off):
                            with_values(e_layer, e_off, beat // 2 - 1)
                        if t.has(m_off):
                            for u in first:
                                for a in (0, 1):
                                    max_scores(m_layer, m_off, u, a)
                        for s in t.steps(slot, beat):
                            step(*s)
                        if t.has(m_off):
                            for u in second:
                                for a in (0, 1):
                                    max_scores(m_layer, m_off, u, a)

            t.run(turn, {-1: lambda: pe.wait_ge(sem["weights_in"], 16),
                         1: lambda: pe.wait_ge(sem["state_weights"], 4)})
            pe.wait_ge(sem["state"], B + 1)
            pe.wait_ge(sem["zo_out1"], 2 * B)
            for i in range(2):
                tokens(DN[:, i, :], "uo", i, lambda kc, tile: c2[:, kc, tile]).then_inc(sem["cu_full"], 1)


N_MEMSETS = 7
N_HALVES = 4
CONSTS = 16 * 12


def queries(layer, kt):
    return 512 - 128 * kt if layer else 512


def keys(layer, qt):
    return 128 * (qt + 1) if layer else 512


def _split(a, dtype):
    import numpy as np
    parts = []
    for _ in range(3):
        p = a.astype(dtype)
        parts.append(p)
        a = a - p.astype(np.float64)
    return parts


def _constants():
    import numpy as np
    bf = mybir.dt.np(mybir.dt.bfloat16)
    H, S = 16, 512
    ratio = 2.0 ** (-8.0 / H)
    slopes = np.array([ratio ** (i + 1) for i in range(H)], np.float32).astype(np.float64)
    line = 4.0 * slopes[:, None] * np.arange(S)[None, :]
    n = ROWS - ROW_EXTRA
    q = np.zeros((2, n, H, S), bf)
    k = np.zeros((n, H, S), bf)
    for i, (kp, qp) in enumerate(zip(_split(line, bf), _split(-line, bf))):
        q[1, i], k[i] = 1.0, kp
        q[1, 3 + i], k[3 + i] = qp, 1.0
    k[ROWS_ALIBI:] = 1.0
    causal = np.where(np.arange(128)[None, :] > np.arange(128)[:, None], -1e30, 0.0).astype(bf)
    return dict(ident_f=np.eye(128, dtype=np.float32), ident_b=np.eye(128).astype(bf), causal=causal,
                extra_q=q, extra_k=k)


def kernel(**inputs):
    import numpy as np
    import concourse.bacc as bacc
    from concourse.bass_utils import run_bass_kernel_spmd

    a = {n: np.asarray(v) for n, v in inputs.items()}
    d_major = np.arange(256).reshape(16, 16).T.reshape(-1)
    weights = np.stack([
        a["L0_attn_Wq"][:, d_major], a["L0_attn_Wk"][:, d_major], a["L0_attn_Wv"], a["L0_attn_Wo"],
        a["L0_ffn_W_r"].T, a["L0_ffn_W_k"].T, a["L0_ffn_W_v"].T,
        a["L1_attn_q_w"][:, d_major], a["L1_attn_k_w"][:, d_major], a["L1_attn_v_w"], a["L1_attn_o_w"],
        a["L1_ffn_wf"].T, a["L1_ffn_uf"].T, a["L1_ffn_wi"].T, a["L1_ffn_ui"].T,
        a["L1_ffn_wc"].T, a["L1_ffn_uc"].T, a["L1_ffn_wo"].T, a["L1_ffn_uo"].T])
    columns = np.stack([a["L0_attn_bq"][d_major], a["L0_attn_bk"][d_major], a["L0_ffn_mu_r"], a["L0_ffn_mu_k"],
                        a["L1_ffn_bf"], a["L1_ffn_bi"], a["L1_ffn_bc"], a["L1_ffn_in_c"]])
    columns = columns.reshape(len(COL_NAMES), 2, 128).transpose(2, 0, 1)
    rows = np.stack([a["L0_attn_bv"], a["L0_attn_bo"], a["L1_ffn_bo"]])
    arrays = dict(x=a["L0_attn_x"], weights=weights, columns=columns, rows=rows, **_constants())
    arrays = {n: np.ascontiguousarray(v) for n, v in arrays.items()}

    nc = bacc.Bacc("TRN2", target_bir_lowering=False, num_devices=1)
    args = [nc.dram_tensor(n, v.shape, mybir.dt.from_np(v.dtype), kind="ExternalInput").ap()
            for n, v in arrays.items()]
    out = nc.dram_tensor("out", arrays["x"].shape, mybir.dt.float32, kind="ExternalOutput").ap()
    sequence_stack_kernel(nc, *args, out)
    result = run_bass_kernel_spmd(nc, [arrays], core_ids=[0])
    return result.results[0]["out"]
```
